# Optimizing a Trainium2 kernel written in Bass

```python
import numpy as np
import jax
import jax.numpy as jnp

def _softmax(x, axis=-1):
    return jax.nn.softmax(x, axis=axis)

def _gelu(x):
    return jax.nn.gelu(x, approximate=True)

def _silu(x):
    return jax.nn.silu(x)

def _sigmoid(x):
    return jax.nn.sigmoid(x)

def _layernorm(x, axis=-1, eps=1e-05):
    m = jnp.mean(x, axis=axis, keepdims=True)
    v = jnp.var(x, axis=axis, keepdims=True)
    return (x - m) / jnp.sqrt(v + eps)

def _scatter_add(tgt, idx, src, axis=0):
    return tgt.at[idx].add(src)

def _segment_sum(src, seg, n):
    return jax.ops.segment_sum(src, seg, n)
kernel_name = 'mk_pixart_resid_d1_seqx_r4_f05788'

def setup_inputs(seed: int=0):
    np.random.seed(seed)
    _w = jnp.asarray

    def _rec_inputs():
        import jax
        import jax.numpy as jnp
        _rk = jax.random.key(seed)
        x = -0.003379 + 0.9984 * jax.random.normal(jax.random.fold_in(_rk, 1), (2, 1024, 256), jnp.float32)
        _lenS = 1024 - jax.random.randint(jax.random.fold_in(_rk, 7), (2,), 0, max(1, 1024 // 4) + 1, jnp.int32)
        _lenS2 = 154 - jax.random.randint(jax.random.fold_in(_rk, 8), (2,), 0, max(1, 154 // 4) + 1, jnp.int32)
        cond_1024 = -0.0142567 + 1.00875 * jax.random.normal(jax.random.fold_in(_rk, 11), (2, 256), jnp.float32)
        _ctx_1024P = jax.random.normal(jax.random.fold_in(_rk, 12), (2, 16, 256), jnp.float32)
        _ctx_1024c = jax.random.dirichlet(jax.random.fold_in(_rk, 512), 0.3 * jnp.ones((16,), jnp.float32), (2, 154))
        _ctx_1024t = jnp.einsum('bsk,bkd->bsd', _ctx_1024c, _ctx_1024P)
        _ctx_1024t = _ctx_1024t * jax.lax.rsqrt(jnp.mean(jnp.square(_ctx_1024t)) + 1e-12) * 0.953939
        ctx_1024 = -5.72187e-05 + 0.999849 * (_ctx_1024t + 0.3 * jax.random.normal(jax.random.fold_in(_rk, 612), (2, 154, 256), jnp.float32))
        return (x, cond_1024, ctx_1024)
    x, cond_1024, ctx_1024 = _rec_inputs()

    def _L0_xcond_setup():
        import jax, jax.numpy as jnp
        import numpy as np
        B, N, K, D, T = (16, 1024, 16, 256, 3)
        EPS_ATTN = 1e-08
        LN_EPS = 1e-05

        def _ln(x, g, b):
            mu = jnp.mean(x, axis=-1, keepdims=True)
            var = jnp.mean(jnp.square(x - mu), axis=-1, keepdims=True)
            return (x - mu) * jax.lax.rsqrt(var + LN_EPS) * g + b
        key = jax.random.key(seed)
        ks = jax.random.split(key, 16)
        w = lambda k, i, o: jax.random.normal(k, (i, o), jnp.float32) * 0.02
        inp = {'x_cls': jax.random.normal(ks[0], (B, D), jnp.float32), 'x': jax.random.normal(ks[1], (B, N, D), jnp.float32), 'noise': jax.random.normal(ks[2], (B, K, D), jnp.float32), 'q_mu': jax.random.normal(ks[3], (1, 1, D), jnp.float32), 'q_logsig': jax.random.normal(ks[4], (1, 1, D), jnp.float32) * 0.02, 'lnkv_g': jnp.ones((D,), jnp.float32), 'lnkv_b': jnp.zeros((D,), jnp.float32), 'lnq_g': jnp.ones((D,), jnp.float32), 'lnq_b': jnp.zeros((D,), jnp.float32), 'lnm_g': jnp.ones((D,), jnp.float32), 'lnm_b': jnp.zeros((D,), jnp.float32), 'lnp_g': jnp.ones((D,), jnp.float32), 'lnp_b': jnp.zeros((D,), jnp.float32), 'wk': w(ks[5], D, D), 'bk': jnp.zeros((D,), jnp.float32), 'wv': w(ks[6], D, D), 'bv': jnp.zeros((D,), jnp.float32), 'wq': w(ks[7], D, D), 'bq': jnp.zeros((D,), jnp.float32), 'wu': w(ks[8], D, D), 'bu': jnp.zeros((D,), jnp.float32), 'w1': w(ks[9], D, D), 'b1': jnp.zeros((D,), jnp.float32), 'w2': w(ks[10], D, D), 'b2': jnp.zeros((D,), jnp.float32)}
        return inp
    _L0_xcond_all = _L0_xcond_setup()
    _L0_xcond_in = {k: v for k, v in _L0_xcond_all.items() if k in ('q_mu', 'q_logsig', 'lnkv_g', 'lnkv_b', 'lnq_g', 'lnq_b', 'lnm_g', 'lnm_b', 'lnp_g', 'lnp_b', 'wk', 'bk', 'wv', 'bv', 'wq', 'bq', 'wu', 'bu', 'w1', 'b1', 'w2', 'b2')}
    del _L0_xcond_all

    def _L0_ffn_setup():
        import jax, jax.numpy as jnp
        import numpy as np
        E = 32
        H = 256
        I = 128
        G = 8
        TKG = 4
        TOPK = 8
        NSH = 2
        SCALE = 2.5
        key = jax.random.key(seed)
        ks = jax.random.split(key, 10)
        s = 0.02
        return {'hidden_states': jax.random.normal(ks[0], (2, 256, H), jnp.float32), 'gate_w': jax.random.normal(ks[1], (E, H), jnp.float32) * s, 'gate_bias': jax.random.normal(ks[2], (E,), jnp.float32) * s, 'w_gate': jax.random.normal(ks[3], (E, I, H), jnp.float32) * s, 'w_up': jax.random.normal(ks[4], (E, I, H), jnp.float32) * s, 'w_down': jax.random.normal(ks[5], (E, H, I), jnp.float32) * s, 'sh_gate': jax.random.normal(ks[6], (I * NSH, H), jnp.float32) * s, 'sh_up': jax.random.normal(ks[7], (I * NSH, H), jnp.float32) * s, 'sh_down': jax.random.normal(ks[8], (H, I * NSH), jnp.float32) * s}
    _L0_ffn_all = _L0_ffn_setup()
    _L0_ffn_in = {k: v for k, v in _L0_ffn_all.items() if k in ('gate_w', 'gate_bias', 'w_gate', 'w_up', 'w_down', 'sh_gate', 'sh_up', 'sh_down')}
    del _L0_ffn_all
    return {'x': x, 'cond_1024': cond_1024, 'ctx_1024': ctx_1024, 'L0_xcond_q_mu': _L0_xcond_in['q_mu'], 'L0_xcond_q_logsig': _L0_xcond_in['q_logsig'], 'L0_xcond_lnkv_g': _L0_xcond_in['lnkv_g'], 'L0_xcond_lnkv_b': _L0_xcond_in['lnkv_b'], 'L0_xcond_lnq_g': _L0_xcond_in['lnq_g'], 'L0_xcond_lnq_b': _L0_xcond_in['lnq_b'], 'L0_xcond_lnm_g': _L0_xcond_in['lnm_g'], 'L0_xcond_lnm_b': _L0_xcond_in['lnm_b'], 'L0_xcond_lnp_g': _L0_xcond_in['lnp_g'], 'L0_xcond_lnp_b': _L0_xcond_in['lnp_b'], 'L0_xcond_wk': _L0_xcond_in['wk'], 'L0_xcond_bk': _L0_xcond_in['bk'], 'L0_xcond_wv': _L0_xcond_in['wv'], 'L0_xcond_bv': _L0_xcond_in['bv'], 'L0_xcond_wq': _L0_xcond_in['wq'], 'L0_xcond_bq': _L0_xcond_in['bq'], 'L0_xcond_wu': _L0_xcond_in['wu'], 'L0_xcond_bu': _L0_xcond_in['bu'], 'L0_xcond_w1': _L0_xcond_in['w1'], 'L0_xcond_b1': _L0_xcond_in['b1'], 'L0_xcond_w2': _L0_xcond_in['w2'], 'L0_xcond_b2': _L0_xcond_in['b2'], 'L0_ffn_gate_w': _L0_ffn_in['gate_w'], 'L0_ffn_gate_bias': _L0_ffn_in['gate_bias'], 'L0_ffn_w_gate': _L0_ffn_in['w_gate'], 'L0_ffn_w_up': _L0_ffn_in['w_up'], 'L0_ffn_w_down': _L0_ffn_in['w_down'], 'L0_ffn_sh_gate': _L0_ffn_in['sh_gate'], 'L0_ffn_sh_up': _L0_ffn_in['sh_up'], 'L0_ffn_sh_down': _L0_ffn_in['sh_down']}

def reference(x, cond_1024, ctx_1024, L0_xcond_q_mu, L0_xcond_q_logsig, L0_xcond_lnkv_g, L0_xcond_lnkv_b, L0_xcond_lnq_g, L0_xcond_lnq_b, L0_xcond_lnm_g, L0_xcond_lnm_b, L0_xcond_lnp_g, L0_xcond_lnp_b, L0_xcond_wk, L0_xcond_bk, L0_xcond_wv, L0_xcond_bv, L0_xcond_wq, L0_xcond_bq, L0_xcond_wu, L0_xcond_bu, L0_xcond_w1, L0_xcond_b1, L0_xcond_w2, L0_xcond_b2, L0_ffn_gate_w, L0_ffn_gate_bias, L0_ffn_w_gate, L0_ffn_w_up, L0_ffn_w_down, L0_ffn_sh_gate, L0_ffn_sh_up, L0_ffn_sh_down):
    import jax
    import jax.numpy as jnp

    def _L0_xcond_ref(x_cls, x, noise, q_mu, q_logsig, lnkv_g, lnkv_b, lnq_g, lnq_b, lnm_g, lnm_b, lnp_g, lnp_b, wk, bk, wv, bv, wq, bq, wu, bu, w1, b1, w2, b2):
        import jax, jax.numpy as jnp
        import numpy as np
        B, N, K, D, T = (16, 1024, 16, 256, 3)
        EPS_ATTN = 1e-08
        LN_EPS = 1e-05

        def _ln(x, g, b):
            mu = jnp.mean(x, axis=-1, keepdims=True)
            var = jnp.mean(jnp.square(x - mu), axis=-1, keepdims=True)
            return (x - mu) * jax.lax.rsqrt(var + LN_EPS) * g + b
        scale = D ** (-0.5)
        x_in = _ln(x, lnkv_g, lnkv_b)
        k = x_in @ wk + bk
        v = x_in @ wv + bv
        slots = q_mu + jnp.exp(q_logsig) * noise
        for _ in range(T):
            prev = slots
            q = _ln(slots, lnq_g, lnq_b) @ wq + bq
            logits = jnp.einsum('bnd,bkd->bnk', k, q) / scale
            attn = jax.nn.softmax(logits, axis=-1) + EPS_ATTN
            attn = attn / jnp.sum(attn, axis=1, keepdims=True)
            upd = jnp.einsum('bnk,bnd->bkd', attn, v)
            slots = upd @ wu + bu + prev
            h = _ln(slots, lnm_g, lnm_b) @ w1 + b1
            slots = jax.nn.gelu(h, approximate=False) @ w2 + b2 + slots
            slots = _ln(slots + x_cls[:, None, :], lnp_g, lnp_b)
        return slots

    def _L0_ffn_ref(hidden_states, gate_w, gate_bias, w_gate, w_up, w_down, sh_gate, sh_up, sh_down):
        import jax, jax.numpy as jnp
        import numpy as np
        E = 32
        H = 256
        I = 128
        G = 8
        TKG = 4
        TOPK = 8
        NSH = 2
        SCALE = 2.5
        B, S, Hd = hidden_states.shape
        h = hidden_states.reshape(-1, Hd)
        logits = h.astype(jnp.float32) @ gate_w.T
        scores = jax.nn.sigmoid(logits)
        sc = scores + gate_bias
        grp = sc.reshape(-1, G, E // G)
        group_scores = jax.lax.top_k(grp, 2)[0].sum(-1)
        gidx = jax.lax.top_k(group_scores, TKG)[1]
        gmask = jnp.sum(jax.nn.one_hot(gidx, G, dtype=sc.dtype), axis=1)
        smask = jnp.repeat(gmask, E // G, axis=1)
        masked = jnp.where(smask > 0, sc, jnp.zeros_like(sc))
        tki = jax.lax.top_k(masked, TOPK)[1]
        tkw = jnp.take_along_axis(scores, tki, axis=1)
        tkw = tkw / (tkw.sum(-1, keepdims=True) + 1e-20)
        tkw = tkw * SCALE
        combine = (jax.nn.one_hot(tki, E, dtype=tkw.dtype) * tkw[..., None]).sum(1)
        g = jax.nn.silu(jnp.einsum('th,eih->tei', h, w_gate))
        u = jnp.einsum('th,eih->tei', h, w_up)
        routed = jnp.einsum('tei,ehi->th', g * u * combine[:, :, None], w_down)
        sg = jax.nn.silu(h @ sh_gate.T)
        shared = sg * (h @ sh_up.T) @ sh_down.T
        return (routed + shared).reshape(B, S, Hd)
    x = x + _L0_xcond_ref(cond_1024, ctx_1024, _layernorm(x, axis=-1), L0_xcond_q_mu, L0_xcond_q_logsig, L0_xcond_lnkv_g, L0_xcond_lnkv_b, L0_xcond_lnq_g, L0_xcond_lnq_b, L0_xcond_lnm_g, L0_xcond_lnm_b, L0_xcond_lnp_g, L0_xcond_lnp_b, L0_xcond_wk, L0_xcond_bk, L0_xcond_wv, L0_xcond_bv, L0_xcond_wq, L0_xcond_bq, L0_xcond_wu, L0_xcond_bu, L0_xcond_w1, L0_xcond_b1, L0_xcond_w2, L0_xcond_b2)
    x = x + _L0_ffn_ref(_layernorm(x, axis=-1), L0_ffn_gate_w, L0_ffn_gate_bias, L0_ffn_w_gate, L0_ffn_w_up, L0_ffn_w_down, L0_ffn_sh_gate, L0_ffn_sh_up, L0_ffn_sh_down)
    return x

_drawn_inputs = setup_inputs


def setup_inputs(seed=0):
    import zlib

    import numpy as np

    out = dict(_drawn_inputs(seed))
    spreads = {'L0_xcond_lnkv_g': (1.0, 0.6),
     'L0_xcond_lnkv_b': (0.0, 0.8),
     'L0_xcond_lnq_g': (1.0, 0.6),
     'L0_xcond_lnq_b': (0.0, 0.8),
     'L0_xcond_lnm_g': (1.0, 0.6),
     'L0_xcond_lnm_b': (0.0, 0.8),
     'L0_xcond_lnp_g': (1.0, 0.2),
     'L0_xcond_lnp_b': (0.0, 0.1),
     'L0_xcond_bk': (0.0, 0.452),
     'L0_xcond_bv': (0.0, 0.385),
     'L0_xcond_bq': (0.0, 0.8),
     'L0_xcond_bu': (0.0, 0.1),
     'L0_xcond_b1': (0.0, 0.732),
     'L0_xcond_b2': (0.0, 0.1)}
    factors = {'L0_xcond_q_logsig': 8.0,
     'L0_ffn_gate_w': 8.0,
     'L0_ffn_gate_bias': 8.0,
     'L0_ffn_w_gate': 8.0,
     'L0_ffn_w_up': 8.0,
     'L0_ffn_w_down': 8.0,
     'L0_ffn_sh_gate': 5.561,
     'L0_ffn_sh_up': 5.251,
     'L0_ffn_sh_down': 5.318}
    for name, (base, spread) in spreads.items():
        noise = np.random.default_rng([zlib.crc32(name.encode()), seed]).standard_normal(out[name].shape)
        drawn = base * np.exp(spread * noise) if base else spread * noise
        out[name] = jnp.asarray(drawn.astype(out[name].dtype))
    for name, factor in factors.items():
        out[name] = (out[name] * factor).astype(out[name].dtype)
    return out
```

```python
from contextlib import ExitStack

import concourse.bass as bass
from concourse import mybir

F32 = mybir.dt.float32
F32R = mybir.dt.float32r
ALU = mybir.AluOpType
ACT = mybir.ActivationFunctionType
AX = mybir.AxisListType

P = 128
BANK = 512
D = 256
DC = D // P
B = 2
S = 1024
T = S // P
Q = S // BANK
TQ = T // Q
N_CTX = 154
NH = N_CTX // 2
J = 2 * B
ROUNDS = 3
SHARPEN = float(D) ** 0.5
LN_EPS = 1e-5
ATTN_EPS = 1e-8
EPS_ROW = 96
VW = D + 2

E = 32
I = 128
SHARED = 2
EG = 8
GE = E // EG
TOPG = 4
TOPK = 8
ROUTE_SCALE = 2.5
LOW = -3.0e38
STRUCK = -2.0e38
WCOL = 3 * D

MATS = ("wk", "wv", "wqT", "wu", "w1", "w2")
COLS = ("bk", "bv", "bq", "lnq_g", "lnq_b", "lnm_g", "lnm_b", "b1")
ROWS = ("lnkv_g", "lnkv_b", "lnp_g", "lnp_b", "bu", "b2", "q_mu", "q_logsig", "cond0", "cond1")


class Lane:

    def __init__(self, engine, sem):
        self.engine, self.sem, self.count, self.seen = engine, sem, 0, {}

    def after(self, *marks):
        for sem, value in marks:
            if self.seen.get(sem.name, 0) < value:
                self.engine.wait_ge(sem, value)
                self.seen[sem.name] = value

    def did(self, instruction):
        instruction.then_inc(self.sem, 1)
        self.count += 1
        return self.sem, self.count


def build(nc, x, ctx_in, rows_in, bias_in, cols_in, mats_in, gate_wT, experts, out, scratch):
    stack = ExitStack()
    with stack:
        def sb(name, shape, dt=F32):
            return stack.enter_context(nc.sbuf_tensor(name, shape, dt))

        def sem(name):
            return stack.enter_context(nc.semaphore(name))

        pe = Lane(nc.tensor, sem("pe_done"))
        act = Lane(nc.scalar, sem("act_done"))
        dve = Lane(nc.vector, sem("dve_done"))
        pool = Lane(nc.gpsimd, sem("pool_done"))
        sync = Lane(nc.sync, sem("sync_unused"))

        xs = sb("xs", [P, B * T, D])
        slots = sb("slots", [P, B * T, D])
        mid = sb("mid", [P, B * T, D])
        hat = sb("hat", [P, B * T, D])
        hatT = [sb(f"hatT{b}", [P, DC, S]) for b in range(B)]
        attn = [sb(f"attn{b}", [P, 2, S]) for b in range(B)]
        gel = [sb(f"gel{b}", [P, DC, S]) for b in range(B)]
        ident = sb("ident", [P, P])
        mats = sb("mats", [P, len(MATS), DC, D])
        w1g = sb("w1g", [P, DC, D])
        rows = sb("rows", [P, len(ROWS), D])
        cols = sb("cols", [P, len(COLS), DC])
        expls = sb("expls", [P, D])

        def part(buffer, at, *dims):
            n = 1
            for d in dims:
                n *= d
            flat = buffer.rearrange("p a b -> p (a b)")[:, at:at + n]
            if len(dims) == 2:
                return flat.rearrange("p (a b) -> p a b", a=dims[0])
            return flat

        ctx = part(gel[1][0:NH, :, :], 0, J, D)
        ctxT = part(gel[1][:, :, :], J * D, DC, J * NH)
        kT, vT, kq_raw = (part(gel[0][:, :, :], i * DC * J * NH, DC, J * NH) for i in range(3))
        kq = sb("kq", [P, DC, J * NH])
        qk_bias = sb("qk_bias", [NH, J])
        b1g = sb("b1g", [P, DC])
        values = sb("values", [NH, J, VW])
        vscaled = [sb(f"vscaled{b}", [P, 2, VW]) for b in range(B)]
        eps_ones = sb("eps_ones", [NH, P])
        stat = sb("stat", [P, B * T, 6])
        mv = sb("mv", [P, B * T, 2])
        var_eps = sb("var_eps", [P, B * T])
        rstd = sb("rstd", [P, B * T])
        minus_half = sb("minus_half", [P, B * T])
        rowmax = sb("rowmax", [NH, J])
        shifted = sb("shifted", [NH, J])
        expbias = sb("expbias", [NH, J])
        rowsum = sb("rowsum", [NH, J])
        rrow = sb("rrow", [NH, J])
        rden = sb("rden", [P, B * T])
        gwT = sb("gwT", [P, DC, E])
        gbias = sb("gbias", [P, E])
        hatT_hi = [sb(f"hatT_hi{b}", [P, DC, S], F32R) for b in range(B)]
        hatT_lo = [sb(f"hatT_lo{b}", [P, DC, S], F32R) for b in range(B)]
        w_hi = [sb(f"w_hi{i}", [P, WCOL], F32R) for i in range(2)]
        w_lo = [sb(f"w_lo{i}", [P, WCOL], F32R) for i in range(2)]
        silu = [part(hat[:, :, :], i * BANK, BANK) for i in range(2)]
        act_in = [part(hat[:, :, :], (2 + i) * BANK, BANK) for i in range(2)]
        act_hi = [sb(f"act_hi{i}", [P, BANK], F32R) for i in range(2)]
        act_lo = [sb(f"act_lo{i}", [P, BANK], F32R) for i in range(2)]
        score = part(mats[:, 0, :, :], 0, T, E)
        biased = part(mats[:, 0, :, :], T * E, T, E)
        pair_hi = sb("pair_hi", [P, T, EG, 2])
        pair_lo = sb("pair_lo", [P, T, EG, 2])
        gtop = sb("gtop", [P, T, EG])
        gsec = sb("gsec", [P, T, EG])
        gscore = sb("gscore", [P, T, EG + TOPG])
        gbest = sb("gbest", [P, T, 8])
        gleft = sb("gleft", [P, T, EG + TOPG])
        gmask = sb("gmask", [P, T, EG])
        masked = part(mats[:, 1, :, :], 0, T, E)
        ebest = sb("ebest", [P, T, 8])
        eleft = part(mats[:, 1, :, :], T * E, T, E)
        chosen = part(mats[:, 2, :, :], 0, T, E)
        wsum = sb("wsum", [P, T])
        wnorm = sb("wnorm", [P, T])
        combine = part(mats[:, 2, :, :], T * E, T, E)
        RAW = 4
        raw = [part(mid[:, :, :], i * WCOL, WCOL) for i in range(RAW)]
        combT = part(mid[0:E, :, :], RAW * WCOL, S)

        ps = stack.enter_context(nc.psum_tensor("ps", [P, 8 * BANK], F32))
        bank_read = [None] * 8

        def bank(i, n=1):
            return ps[:, i * BANK:(i + n) * BANK]

        def mat(name, c):
            return mats[:, MATS.index(name), c, :]

        def row(name, p=P):
            return rows[0:p, ROWS.index(name), :]

        def col(name, c):
            i = COLS.index(name)
            return cols[:, i, c:c + 1]

        def pe_bank(i):
            if bank_read[i] is not None:
                pe.after(bank_read[i])

        def load(eng, name, dst, src):
            s = sem(name)
            eng.dma_start(dst, src).then_inc(s, 16)
            return s, 16

        ctx_in_sb = load(nc.sync, "ld_ctx", ctx[:, :, :], ctx_in.rearrange("b (h n) d -> n (b h) d", h=2))
        mats_in_sb = load(nc.sync, "ld_mats", mats[:, 0:4, :, :], mats_in[:, 0:4, :, :])
        x_in_sb = []
        for b in range(B):
            x_in_sb.append(load(nc.sync, f"ld_x{b}", xs[:, b * T:(b + 1) * T, :],
                                x[b].rearrange("(t p) d -> p t d", p=P)))
        mats2_in_sb = load(nc.sync, "ld_mats2", mats[:, 4:6, :, :], mats_in[:, 4:6, :, :])
        gwT_in_sb = load(nc.sync, "ld_gw", gwT[:, :, :], gate_wT)
        rows_in_sb = load(nc.scalar, "ld_rows", rows[:, :, :].rearrange("p r d -> p (r d)"),
                          rows_in.to_broadcast([P, len(ROWS) * D]))
        cols_in_sb = load(nc.scalar, "ld_cols", cols[:, :, :], cols_in)
        gbias_in_sb = load(nc.scalar, "ld_gb", gbias[:, :], bias_in.to_broadcast([P, E]))

        ident0 = pool.did(nc.gpsimd.memset(ident[:, :], 0.0))
        pool.after(ident0)
        identity = pool.did(nc.gpsimd.affine_select(
            out=ident[:, :], in_=ident[:, :], compare_op=ALU.not_equal, fill=1.0, base=0,
            pattern=[[-1, P]], channel_multiplier=1))
        half_set = pool.did(nc.gpsimd.memset(minus_half[:, :], -0.5))
        for b in range(B):
            pool.did(nc.gpsimd.memset(vscaled[b][:, :, :], 0.0))
            pool.did(nc.gpsimd.memset(attn[b][:, 0, :], 1.0))
        pool_constants = (pool.sem, pool.count)
        dve.did(nc.vector.memset(eps_ones[:, :], ATTN_EPS))
        constants = dve.did(nc.vector.memset(values[:, :, D:VW], 1.0))

        def norm_stats(tiles, source, parts=P):
            for g in tiles:
                last = dve.did(nc.vector.bn_stats(stat[0:parts, g, :], source(g)))
            dve.after(last)
            for g in tiles:
                last = dve.did(nc.vector.bn_aggr(mv[0:parts, g, :], stat[0:parts, g, :]))
            dve.after(last)
            a, z = tiles[0], tiles[-1] + 1
            var = dve.did(nc.vector.tensor_scalar_add(var_eps[0:parts, a:z], mv[0:parts, a:z, 1], LN_EPS))
            pool.after(var, half_set)
            return pool.did(nc.gpsimd.tensor_tensor(rstd[0:parts, a:z], var_eps[0:parts, a:z],
                                                    minus_half[0:parts, a:z], ALU.pow))

        def norm_apply(tiles, source, dest, scaled, parts=P):
            dve.after(scaled)
            return [dve.did(nc.vector.tensor_scalar(dest(g), source(g), mv[0:parts, g, 0:1],
                                                    rstd[0:parts, g:g + 1], ALU.subtract, ALU.mult))
                    for g in tiles]

        def norm_affine(tiles, source, dest, scaled, gain, shift):
            dve.after(scaled)
            marks = [dve.did(nc.vector.scalar_tensor_tensor(
                out=dest(g), in0=source(g), scalar=mv[:, g, 0:1], in1=gain,
                op0=ALU.subtract, op1=ALU.mult)) for g in tiles]
            last = None
            for g, m in zip(tiles, marks):
                dve.after(m)
                last = dve.did(nc.vector.scalar_tensor_tensor(
                    out=dest(g), in0=dest(g), scalar=rstd[:, g:g + 1], in1=shift,
                    op0=ALU.mult, op1=ALU.add))
            return last

        def transpose_block(b, q, source, ready, banks):
            marks = []
            for dc in range(DC):
                pe_bank(banks[dc])
            for i in range(TQ):
                g = b * T + q * TQ + i
                pe.after(ready[i])
                for dc in range(DC):
                    last = nc.tensor.transpose(bank(banks[dc])[:, i * P:(i + 1) * P],
                                               source(g)[:, dc * P:(dc + 1) * P], ident[:, :])
                    if i == TQ - 1:
                        marks.append(pe.did(last))
            return marks

        pe.after(identity)
        dve.after(ctx_in_sb)
        ctx_norm = norm_stats(list(range(J)), lambda j: ctx[:, j, :], NH)
        last = norm_apply(list(range(J)), lambda j: ctx[:, j, :], lambda j: ctx[:, j, :], ctx_norm, NH)
        dve.after(rows_in_sb, *last)
        last = [dve.did(nc.vector.tensor_tensor(ctx[:, j, :], ctx[:, j, :], row("lnkv_g", NH), ALU.mult))
                for j in range(J)]
        dve.after(*last)
        ctx_ready = [dve.did(nc.vector.tensor_tensor(ctx[:, j, :], ctx[:, j, :], row("lnkv_b", NH), ALU.add))
                     for j in range(J)]
        for dc in range(DC):
            for j in range(J):
                pe.after(ctx_ready[j])
                last = nc.tensor.transpose(bank(dc)[:, j * NH:(j + 1) * NH],
                                           ctx[:, j, dc * P:(dc + 1) * P], ident[0:NH, 0:NH])
            act.after(pe.did(last))
            ctxT_ready = bank_read[dc] = act.did(nc.scalar.copy(ctxT[:, dc, :], bank(dc)[:, 0:J * NH]))

        def project(bank0, weights, moving, n=J * NH):
            marks = []
            for oc in range(DC):
                pe_bank(bank0 + oc)
                for ic in range(DC):
                    last = nc.tensor.matmul(bank(bank0 + oc)[:, 0:n], weights(ic)[:, oc * P:(oc + 1) * P],
                                            moving(ic), start=ic == 0, stop=ic == DC - 1)
                marks.append(pe.did(last))
            return marks

        pe.after(ctxT_ready, mats_in_sb)
        k_sum = project(2, lambda c: mat("wk", c), lambda c: ctxT[:, c, :])
        v_sum = project(4, lambda c: mat("wv", c), lambda c: ctxT[:, c, :])
        dve.after(cols_in_sb)
        for oc in range(DC):
            dve.after(k_sum[oc])
            k_ready = bank_read[2 + oc] = dve.did(nc.vector.tensor_scalar_add(
                kT[:, oc, :], bank(2 + oc)[:, 0:J * NH], col("bk", oc)))
        for oc in range(DC):
            dve.after(v_sum[oc])
            v_ready = bank_read[4 + oc] = dve.did(nc.vector.tensor_scalar_add(
                vT[:, oc, :], bank(4 + oc)[:, 0:J * NH], col("bv", oc)))
        pe.after(k_ready)
        kq_sum = project(6, lambda c: mat("wqT", c), lambda c: kT[:, c, :])
        for dc in range(DC):
            dve.after(kq_sum[dc])
            dve.did(nc.vector.tensor_copy(kq_raw[:, dc, :], bank(6 + dc)[:, 0:J * NH]))
            kq_ready = bank_read[6 + dc] = dve.did(nc.vector.tensor_scalar(
                kq[:, dc, :], bank(6 + dc)[:, 0:J * NH], col("lnq_g", dc), None, ALU.mult))
        pe.after(v_ready)
        pe.after(constants)
        for j in range(J):
            pe_bank(j % 2)
            for dc in range(DC):
                last = nc.tensor.matmul(bank(j % 2)[0:NH, 0:D], vT[:, dc, j * NH:(j + 1) * NH], mat("wu", dc),
                                        start=dc == 0, stop=dc == DC - 1)
            dve.after(pe.did(last))
            values_ready = bank_read[j % 2] = dve.did(nc.vector.tensor_tensor(
                values[:, j, 0:D], bank(j % 2)[0:NH, 0:D], row("bu", NH), ALU.add))
        pe.after(values_ready)
        dve.after(pool_constants)
        act.after(pool_constants)
        for b in range(B):
            pe_bank(2 + b)
            for h in range(2):
                last = nc.tensor.matmul(bank(2 + b)[:, 0:D + 1], eps_ones[:, :], values[:, 2 * b + h, 0:D + 1],
                                        start=h == 0, stop=h == 1)
            dve.after(pe.did(last))
            eps_row_ready = bank_read[2 + b] = dve.did(nc.vector.tensor_copy(
                vscaled[b][EPS_ROW:EPS_ROW + 1, 0, 0:D + 1], bank(2 + b)[EPS_ROW:EPS_ROW + 1, 0:D + 1]))
        pe.after(kq_ready, cols_in_sb)
        pe_bank(4)
        for j in range(J):
            pairs = [(kq_raw, "lnq_b", c) for c in range(DC)] + [(kT, "bq", c) for c in range(DC)]
            for i, (left, name, c) in enumerate(pairs):
                last = nc.tensor.matmul(bank(4)[0:NH, j:j + 1], left[:, c, j * NH:(j + 1) * NH], col(name, c),
                                        start=i == 0, stop=i == len(pairs) - 1)
        dve.after(pe.did(last))
        qk_bias_ready = bank_read[4] = dve.did(nc.vector.tensor_copy(qk_bias[:, :], bank(4)[0:NH, 0:J]))
        dve.after(mats2_in_sb)
        for dc in range(DC):
            w1g_ready = dve.did(nc.vector.tensor_scalar(w1g[:, dc, :], mat("w1", dc), col("lnm_g", dc), None,
                                                        ALU.mult))
        pe.after(mats2_in_sb)
        pe_bank(5)
        for fc in range(DC):
            for dc in range(DC):
                last = nc.tensor.matmul(bank(5)[:, fc:fc + 1], mat("w1", dc)[:, fc * P:(fc + 1) * P],
                                        col("lnm_b", dc), start=dc == 0, stop=dc == DC - 1)
        dve.after(pe.did(last))
        b1g_ready = bank_read[5] = dve.did(nc.vector.tensor_tensor(
            b1g[:, :], bank(5)[:, 0:DC], cols[:, COLS.index("b1"), :], ALU.add))
        for b in range(B):
            cond_ready = dve.did(nc.vector.tensor_tensor(row(f"cond{b}"), row(f"cond{b}"), row("b2"), ALU.add))
        act.after(rows_in_sb)
        expls_ready = act.did(nc.scalar.activation(expls[:, :], row("q_logsig"), ACT.Exp))

        slots_ready = [None] * B
        for b in range(B):
            tiles = list(range(b * T, (b + 1) * T))
            dve.after(x_in_sb[b])
            scaled = norm_stats(tiles, lambda g: xs[:, g, :])
            dve.after(expls_ready)
            slots_ready[b] = norm_affine(tiles, lambda g: xs[:, g, :], lambda g: slots[:, g, :], scaled,
                                         expls[:, :], row("q_mu"))

        hatT_ready = [[None] * Q for _ in range(B)]
        vscaled_ready = [None] * B
        exp_done = [None] * B
        attended = [[None] * T for _ in range(B)]
        gelu_ready = [[None] * Q for _ in range(B)]

        def evacuate(b, q, marks, banks, dest):
            act.after(marks[0])
            m0 = bank_read[banks[0]] = act.did(nc.scalar.copy(
                dest[:, 0, q * BANK:(q + 1) * BANK], bank(banks[0])))
            act.after(marks[1])
            m1 = bank_read[banks[1]] = act.did(nc.scalar.copy(
                dest[:, 1, q * BANK:(q + 1) * BANK], bank(banks[1])))
            return [m0, m1]

        def normalise_queries(b):
            for q in range(Q):
                tiles = [b * T + q * TQ + i for i in range(TQ)]
                dve.after(slots_ready[b])
                scaled = norm_stats(tiles, lambda g: slots[:, g, :])
                ready = norm_apply(tiles, lambda g: slots[:, g, :], lambda g: hat[:, g, :], scaled)
                banks = [4 * b + 2 * q, 4 * b + 2 * q + 1]
                marks = transpose_block(b, q, lambda g: hat[:, g, :], ready, banks)
                hatT_ready[b][q] = evacuate(b, q, marks, banks, hatT[b])

        def attend(b):
            for h in range(2):
                j = 2 * b + h
                for q in range(Q):
                    i = 4 * b + 2 * h + q
                    pe_bank(i)
                    pe.after(*hatT_ready[b][q])
                    for dc in range(DC):
                        last = nc.tensor.matmul(bank(i)[0:NH, :], kq[:, dc, j * NH:(j + 1) * NH],
                                                hatT[b][:, dc, q * BANK:(q + 1) * BANK],
                                                start=dc == 0, stop=dc == DC - 1)
                logits_ready = pe.did(last)
                logits = bank(4 * b + 2 * h, 2)[0:NH, :]
                dve.after(logits_ready)
                m = dve.did(nc.vector.reduce_max(rowmax[:, j:j + 1], logits, AX.X))
                dve.after(m)
                m = dve.did(nc.vector.tensor_tensor(shifted[:, j:j + 1], rowmax[:, j:j + 1],
                                                    qk_bias[:, j:j + 1], ALU.add))
                dve.after(m)
                m = dve.did(nc.vector.tensor_scalar(expbias[:, j:j + 1], qk_bias[:, j:j + 1],
                                                    shifted[:, j:j + 1], SHARPEN, ALU.subtract, ALU.mult))
                act.after(m)
                e = act.did(nc.scalar.activation(attn[b][0:NH, h, :], logits, ACT.Exp,
                                                 bias=expbias[:, j:j + 1], scale=SHARPEN,
                                                 accum_out=rowsum[:, j:j + 1]))
                exp_done[b] = bank_read[4 * b + 2 * h] = bank_read[4 * b + 2 * h + 1] = e
                dve.after(e)
                m = dve.did(nc.vector.reciprocal(rrow[:, j:j + 1], rowsum[:, j:j + 1]))
                dve.after(m)
                vscaled_ready[b] = dve.did(nc.vector.tensor_scalar(
                    vscaled[b][0:NH, h, :], values[:, j, :], rrow[:, j:j + 1], None, ALU.mult))

        def update(b):
            pe.after(vscaled_ready[b], exp_done[b])
            for t in range(T):
                g = b * T + t
                i = 4 * b + t % 4
                pe_bank(i)
                for h in range(2):
                    k = EPS_ROW + 1 if h == 0 else NH
                    last = nc.tensor.matmul(bank(i)[:, 0:D + 1], attn[b][0:k, h, t * P:(t + 1) * P],
                                            vscaled[b][0:k, h, 0:D + 1], start=h == 0, stop=h == 1)
                dve.after(pe.did(last))
                dve.after(dve.did(nc.vector.reciprocal(rden[:, g:g + 1], bank(i)[:, D:D + 1])))
                attended[b][t] = bank_read[i] = dve.did(nc.vector.scalar_tensor_tensor(
                    out=mid[:, g, :], in0=bank(i)[:, 0:D], scalar=rden[:, g:g + 1], in1=slots[:, g, :],
                    op0=ALU.mult, op1=ALU.add))
            for q in range(Q):
                tiles = [b * T + q * TQ + i for i in range(TQ)]
                dve.after(attended[b][q * TQ + TQ - 1])
                scaled = norm_stats(tiles, lambda g: mid[:, g, :])
                ready = norm_apply(tiles, lambda g: mid[:, g, :], lambda g: hat[:, g, :], scaled)
                pool.after(ready[-1], cond_ready)
                for g in tiles:
                    conditioned[g] = pool.did(nc.gpsimd.tensor_tensor(mid[:, g, :], mid[:, g, :],
                                                                      row(f"cond{b}"), ALU.add))
                banks = [4 * b + 2 * q, 4 * b + 2 * q + 1]
                marks = transpose_block(b, q, lambda g: hat[:, g, :], ready, banks)
                hatT_ready[b][q] = evacuate(b, q, marks, banks, hatT[b])

        conditioned = {}

        def mlp_in(b):
            for q in range(Q):
                pe.after(*hatT_ready[b][q])
                for fc in range(DC):
                    i = 4 * b + 2 * q + fc
                    pe_bank(i)
                    for dc in range(DC):
                        last = nc.tensor.matmul(bank(i), w1g[:, dc, fc * P:(fc + 1) * P],
                                                hatT[b][:, dc, q * BANK:(q + 1) * BANK],
                                                start=dc == 0, stop=dc == DC - 1)
                    act.after(pe.did(last), b1g_ready)
                    gelu_ready[b][q] = bank_read[i] = act.did(nc.scalar.activation(
                        gel[b][:, fc, q * BANK:(q + 1) * BANK], bank(i), ACT.Gelu, bias=b1g[:, fc:fc + 1]))

        def mlp_out(b):
            for q in range(Q):
                pe.after(gelu_ready[b][q])
                tiles = [b * T + q * TQ + i for i in range(TQ)]
                for i in range(TQ // 2):
                    k = 4 * b + 2 * q + i
                    pe_bank(k)
                    for t in range(2):
                        g = tiles[2 * i + t]
                        s = (g - b * T) * P
                        for fc in range(DC):
                            last = nc.tensor.matmul(bank(k)[:, t * D:(t + 1) * D], gel[b][:, fc, s:s + P],
                                                    mat("w2", fc), start=fc == 0, stop=fc == DC - 1)
                    g = tiles[2 * i]
                    dve.after(pe.did(last), conditioned[g + 1])
                    last = bank_read[k] = dve.did(nc.vector.tensor_tensor(
                        mid[:, g:g + 2, :], bank(k).rearrange("p (t d) -> p t d", t=2),
                        mid[:, g:g + 2, :], ALU.add))
                dve.after(last)
                scaled = norm_stats(tiles, lambda g: mid[:, g, :])
                slots_ready[b] = norm_affine(tiles, lambda g: mid[:, g, :], lambda g: slots[:, g, :], scaled,
                                             row("lnp_g"), row("lnp_b"))

        pe.after(w1g_ready, eps_row_ready)
        dve.after(qk_bias_ready)
        stages = [normalise_queries, attend, update, mlp_in, mlp_out] * ROUNDS
        LAG = 2
        for n in range(len(stages) + LAG):
            if n < len(stages):
                stages[n](0)
            if n >= LAG:
                stages[n - LAG](1)

        x1T = attn
        x1T_ready = [None] * B
        split_ready = [[None] * Q for _ in range(B)]
        weights_stored = [None] * B
        pool_s = dve.did(nc.vector.memset(gscore[:, :, EG:], LOW))
        dve.after(pool_s)
        for b in range(B):
            tiles = list(range(b * T, (b + 1) * T))
            dve.after(slots_ready[b])
            last = dve.did(nc.vector.tensor_tensor(xs[:, b * T:(b + 1) * T, :], xs[:, b * T:(b + 1) * T, :],
                                                   slots[:, b * T:(b + 1) * T, :], ALU.add))
            dve.after(last)
            scaled = norm_stats(tiles, lambda g: xs[:, g, :])
            ready = norm_apply(tiles, lambda g: xs[:, g, :], lambda g: hat[:, g, :], scaled)
            for q in range(Q):
                banks = [4 * b + 2 * q, 4 * b + 2 * q + 1]
                marks = transpose_block(b, q, lambda g: hat[:, g, :], ready[q * TQ:], banks)
                for dc in range(DC):
                    span = slice(q * BANK, (q + 1) * BANK)
                    act.after(marks[dc])
                    act.did(nc.scalar.copy(hatT_hi[b][:, dc, span], bank(banks[dc])))
                    m = bank_read[banks[dc]] = act.did(nc.scalar.copy(hatT[b][:, dc, span], bank(banks[dc])))
                    dve.after(m)
                    split_ready[b][q] = dve.did(nc.vector.tensor_tensor(
                        hatT_lo[b][:, dc, span], hatT[b][:, dc, span], hatT_hi[b][:, dc, span].bitcast(F32),
                        ALU.subtract))
                marks = transpose_block(b, q, lambda g: xs[:, g, :], [last] * TQ, banks)
                x1T_ready[b] = evacuate(b, q, marks, banks, x1T[b])
            pe_bank(4 * b)
            pe.after(gwT_in_sb)
            for t in range(T):
                for dc in range(DC):
                    last = nc.tensor.matmul(bank(4 * b)[:, t * E:(t + 1) * E], hatT[b][:, dc, t * P:(t + 1) * P],
                                            gwT[:, dc, :], start=dc == 0, stop=dc == DC - 1)
            act.after(pe.did(last))
            if b:
                act.after(weights_stored[0])
            m = bank_read[4 * b] = act.did(nc.scalar.activation(
                score[:, :, :], bank(4 * b)[:, 0:T * E].rearrange("p (t e) -> p t e", e=E), ACT.Sigmoid))
            dve.after(m, gbias_in_sb)

            def step(instruction):
                m = dve.did(instruction)
                dve.after(m)
                return m

            step(nc.vector.tensor_tensor(biased[:, :, :], score[:, :, :],
                                         gbias[:, :].rearrange("p (o e) -> p o e", o=1).to_broadcast([P, T, E]),
                                         ALU.add))
            four = biased[:, :, :].rearrange("p t (g u v) -> p (t g) u v", g=EG, u=2)
            hi4 = pair_hi[:, :, :, :].rearrange("p t g u -> p (t g) u")
            lo4 = pair_lo[:, :, :, :].rearrange("p t g u -> p (t g) u")
            top, sec = (a[:, :, :].rearrange("p t g -> p (t g)") for a in (gtop, gsec))
            dve.did(nc.vector.tensor_tensor(hi4, four[:, :, :, 0], four[:, :, :, 1], ALU.max))
            step(nc.vector.tensor_tensor(lo4, four[:, :, :, 0], four[:, :, :, 1], ALU.min))
            dve.did(nc.vector.tensor_tensor(top, hi4[:, :, 0], hi4[:, :, 1], ALU.max))
            dve.did(nc.vector.tensor_tensor(sec, hi4[:, :, 0], hi4[:, :, 1], ALU.min))
            step(nc.vector.tensor_tensor(lo4[:, :, 0], lo4[:, :, 0], lo4[:, :, 1], ALU.max))
            step(nc.vector.tensor_tensor(sec, sec, lo4[:, :, 0], ALU.max))
            step(nc.vector.tensor_tensor(gscore[:, :, 0:EG], gtop[:, :, :], gsec[:, :, :], ALU.add))
            for t in range(T):
                m = dve.did(nc.vector.max(gbest[:, t, :], gscore[:, t, :]))
            dve.after(m)
            step(nc.vector.memset(gbest[:, :, TOPG:], LOW))
            for t in range(T):
                m = dve.did(nc.vector.match_replace(gleft[:, t, :], gbest[:, t, :], gscore[:, t, :], STRUCK))
            dve.after(m)
            step(nc.vector.tensor_tensor(gmask[:, :, :], gleft[:, :, 0:EG], gscore[:, :, 0:EG], ALU.not_equal))
            step(nc.vector.tensor_tensor(
                masked[:, :, :].rearrange("p t (g v) -> p (t g) v", g=EG),
                biased[:, :, :].rearrange("p t (g v) -> p (t g) v", g=EG),
                gmask[:, :, :].rearrange("p t (g o) -> p (t g) o", o=1).to_broadcast([P, T * EG, GE]), ALU.mult))
            for t in range(T):
                m = dve.did(nc.vector.max(ebest[:, t, :], masked[:, t, :]))
            dve.after(m)
            for t in range(T):
                m = dve.did(nc.vector.match_replace(eleft[:, t, :], ebest[:, t, :], masked[:, t, :], LOW))
            dve.after(m)
            step(nc.vector.tensor_tensor(chosen[:, :, :], eleft[:, :, :], masked[:, :, :], ALU.not_equal))
            step(nc.vector.tensor_tensor(chosen[:, :, :], chosen[:, :, :], score[:, :, :], ALU.mult))
            step(nc.vector.reduce_sum(wsum[:, :], chosen[:, :, :], AX.X))
            step(nc.vector.tensor_scalar_add(wsum[:, :], wsum[:, :], 1e-20))
            step(nc.vector.reciprocal(wnorm[:, :], wsum[:, :]))
            step(nc.vector.tensor_scalar(wnorm[:, :], wnorm[:, :], ROUTE_SCALE, None, ALU.mult))
            m = step(nc.vector.tensor_tensor(
                combine[:, :, :], chosen[:, :, :],
                wnorm[:, :].rearrange("p (t o) -> p t o", o=1).to_broadcast([P, T, E]), ALU.mult))
            pe.after(m)
            pe_bank(4 * b + 2)
            pe_bank(4 * b + 3)
            for t in range(T):
                last = nc.tensor.transpose(bank(4 * b + 2, 2)[0:E, t * P:(t + 1) * P], combine[:, t, :], ident[:, :])
            act.after(pe.did(last))
            m = bank_read[4 * b + 2] = bank_read[4 * b + 3] = act.did(
                nc.scalar.copy(combT[:, :], bank(4 * b + 2, 2)[0:E, :]))
            act.after(m)
            s = sem(f"st_comb{b}")
            nc.scalar.dma_start(scratch[b], combT[:, :]).then_inc(s, 16)
            weights_stored[b] = (s, 16)

        CW = 4
        cweight = [gel[i // 2][:, i % 2, :] for i in range(CW)]
        raw_sem = [sem(f"ld_w{i}") for i in range(RAW)]
        cw_sem = [sem(f"ld_c{i}") for i in range(CW)]
        split_w = [None] * RAW
        cw_read = [None] * CW
        w_read = [None] * 2
        EXPERTS = E + SHARED
        order = [(b, e) for b in range(B) for e in range(EXPERTS)]
        mid_free = slots_ready
        w_count = c_count = 0
        w_loaded, c_loaded = {}, {}

        def load_expert(n):
            nonlocal w_count, c_count
            b, e = order[n]
            i = w_count % RAW
            sync.after(*(mid_free if split_w[i] is None else [split_w[i]]))
            nc.sync.dma_start(raw[i], experts[e]).then_inc(raw_sem[i], 16)
            w_loaded[n] = (i, (raw_sem[i], 16 * (w_count // RAW + 1)))
            w_count += 1
            if e < E:
                i = c_count % CW
                sync.after(weights_stored[b], *(mid_free if cw_read[i] is None else [cw_read[i]]))
                nc.sync.dma_start(cweight[i], scratch[b, e:e + 1, :].to_broadcast([P, S])).then_inc(cw_sem[i], 16)
                c_loaded[n] = (i, (cw_sem[i], 16 * (c_count // CW + 1)))
                c_count += 1

        w_ready = {}

        def split_weights(n):
            i, loaded = w_loaded[n]
            act.after(loaded)
            if w_read[n % 2] is not None:
                act.after(w_read[n % 2])
            hi = act.did(nc.scalar.copy(w_hi[n % 2][:, :], raw[i]))
            dve.after(hi, loaded)
            w_ready[n] = split_w[i] = dve.did(nc.vector.tensor_tensor(
                w_lo[n % 2][:, :], raw[i], w_hi[n % 2][:, :].bitcast(F32), ALU.subtract))

        def three_passes(dest, left, right, first, final):
            terms = [(a, c) for (lh, ll), (rh, rl) in zip(left, right) for a, c in ((lh, rh), (lh, rl), (ll, rh))]
            for k, (a, c) in enumerate(terms):
                last = nc.tensor.matmul(dest, a, c, start=first and k == 0, stop=final and k == len(terms) - 1)
            return last

        blocks = [(n, q) for n in range(len(order)) for q in range(Q)]
        up_done, gate_done, inner_ready = {}, {}, {}
        down_done = {}

        def gate_up(m):
            n, q = blocks[m]
            b, e = order[n]
            hi, lo = w_hi[n % 2], w_lo[n % 2]
            pe.after(w_ready[n], split_ready[b][q])
            span = slice(q * BANK, (q + 1) * BANK)
            for which, done in ((0, gate_done), (1, up_done)):
                i = 4 + 2 * (m % 2) + which
                pe_bank(i)
                o = [which * D + dc * P for dc in range(DC)]
                done[m] = pe.did(three_passes(
                    bank(i), [(hi[:, a:a + P], lo[:, a:a + P]) for a in o],
                    [(hatT_hi[b][:, dc, span], hatT_lo[b][:, dc, span]) for dc in range(DC)], True, True))

        def gated(m):
            n, q = blocks[m]
            b, e = order[n]
            u = m % 2
            act.after(gate_done[m])
            if m >= 2:
                act.after(inner_ready[m - 2])
            s = bank_read[4 + 2 * u] = act.did(nc.scalar.activation(silu[u][:, :], bank(4 + 2 * u), ACT.Silu))
            dve.after(s)
            if e < E:
                i, loaded = c_loaded[n]
                dve.after(loaded)
                cw_read[i] = dve.did(nc.vector.tensor_tensor(
                    silu[u][:, :], silu[u][:, :], cweight[i][:, q * BANK:(q + 1) * BANK], ALU.mult))
                dve.after(cw_read[i])
            dve.after(up_done[m])
            v = bank_read[5 + 2 * u] = dve.did(nc.vector.tensor_tensor(
                act_in[u][:, :], bank(5 + 2 * u), silu[u][:, :], ALU.mult))
            dve.after(v)
            if m >= 2:
                dve.after(down_done[m - 2])
            h = dve.did(nc.vector.tensor_copy(act_hi[u][:, :], act_in[u][:, :]))
            dve.after(h)
            inner_ready[m] = dve.did(nc.vector.tensor_tensor(
                act_lo[u][:, :], act_in[u][:, :], act_hi[u][:, :].bitcast(F32), ALU.subtract))

        def down(m):
            n, q = blocks[m]
            b, e = order[n]
            u = m % 2
            pe.after(inner_ready[m])
            for dc in range(DC):
                i = 2 * dc + q
                if e == 0:
                    pe_bank(i)
                a = 2 * D + dc * P
                last = three_passes(bank(i), [(w_hi[n % 2][:, a:a + P], w_lo[n % 2][:, a:a + P])],
                                    [(act_hi[u][:, :], act_lo[u][:, :])], e == 0, e == EXPERTS - 1)
            down_done[m] = pe.did(last)
            if q == Q - 1:
                w_read[n % 2] = down_done[m]
            if q == Q - 1 and e == EXPERTS - 1:
                finish(b)

        stored = []

        def finish(b):
            dve.after(*x1T_ready[b], down_done[Q * ((b + 1) * EXPERTS) - 1])
            for q in range(Q):
                for dc in range(DC):
                    span = slice(q * BANK, (q + 1) * BANK)
                    m = bank_read[2 * dc + q] = dve.did(nc.vector.tensor_tensor(
                        hatT[b][:, dc, span], bank(2 * dc + q), x1T[b][:, dc, span], ALU.add))
                sync.after(m)
                s = sem(f"st_out{b}{q}")
                nc.sync.dma_start(out[b, :, :, q * BANK:(q + 1) * BANK].rearrange("c p s -> p c s"),
                                  hatT[b][:, :, span]).then_inc(s, 16)
                stored.append((s, 16))

        AHEAD = 3
        for n in range(AHEAD):
            load_expert(n)
        split_weights(0)
        gate_up(0)
        for m in range(len(blocks)):
            n, q = blocks[m]
            if q == 0 and n + AHEAD < len(order):
                load_expert(n + AHEAD)
            gated(m)
            if q == 0 and n + 1 < len(order):
                split_weights(n + 1)
            if m + 1 < len(blocks):
                gate_up(m + 1)
            down(m)
        sync.after(*stored, *weights_stored)


def kernel(**inputs):
    import numpy as np
    import concourse.bacc as bacc
    from concourse.bass_utils import run_bass_kernel_spmd

    a = {k.replace("L0_xcond_", "").replace("L0_ffn_", ""): np.asarray(v) for k, v in inputs.items()}
    chunked = lambda w: w.reshape(DC, P, -1).transpose(1, 0, 2)
    a["wqT"] = a["wq"].T
    a["cond0"], a["cond1"] = a["cond_1024"]
    mats = np.stack([chunked(a[n]) for n in MATS], axis=1)
    cols = np.stack([a[n].reshape(DC, P).T for n in COLS], axis=1)
    rows = np.concatenate([a[n].reshape(1, D) for n in ROWS], axis=1)

    def expert(gate, up, down):
        return np.concatenate([chunked(gate.T).reshape(P, D), chunked(up.T).reshape(P, D), down.T], axis=1)

    experts = np.stack(
        [expert(a["w_gate"][e], a["w_up"][e], a["w_down"][e]) for e in range(E)]
        + [expert(a["sh_gate"][s:s + I], a["sh_up"][s:s + I], a["sh_down"][:, s:s + I])
           for s in range(0, SHARED * I, I)])
    arrays = {
        "x": a["x"], "ctx": a["ctx_1024"], "rows": rows, "gate_bias": a["gate_bias"].reshape(1, E), "cols": cols,
        "mats": mats, "gate_wT": chunked(a["gate_w"].T), "experts": experts,
    }
    arrays = {k: np.ascontiguousarray(v) for k, v in arrays.items()}
    nc = bacc.Bacc("TRN2", target_bir_lowering=False, num_devices=1)
    args = [nc.dram_tensor(f"in_{n}", v.shape, F32, kind="ExternalInput").ap() for n, v in arrays.items()]
    out = nc.dram_tensor("out", (B, DC, P, S), F32, kind="ExternalOutput").ap()
    scratch = nc.dram_tensor("routing", (B, E, S), F32, kind="Internal").ap()
    build(nc, *args, out, scratch)
    got = run_bass_kernel_spmd(nc, [{f"in_{n}": v for n, v in arrays.items()}], core_ids=[0]).results[0]["out"]
    return np.ascontiguousarray(got.reshape(B, D, S).transpose(0, 2, 1))
```

```python
from contextlib import ExitStack

import concourse.bass as bass
from concourse import mybir

F32 = mybir.dt.float32
F32R = mybir.dt.float32r
ALU = mybir.AluOpType
ACT = mybir.ActivationFunctionType
AX = mybir.AxisListType

P = 128
BANK = 512
D = 256
DC = D // P
B = 2
S = 1024
T = S // P
Q = S // BANK
TQ = T // Q
N_CTX = 154
NH = N_CTX // 2
J = 2 * B
ROUNDS = 3
BATCH_LAG_US = 20
BLOCK_LAG_US = 3
HANDOVER_US = 0.2
SHARPEN = float(D) ** 0.5
LN_EPS = 1e-5
ATTN_EPS = 1e-8
EPS_ROW = 96
VW = D + 2

E = 32
I = 128
SHARED = 2
EG = 8
GE = E // EG
TOPG = 4
TOPK = 8
ROUTE_SCALE = 2.5
LOW = -3.0e38
STRUCK = -2.0e38
WCOL = 3 * D

MATS = ("wk", "wv", "wqT", "wu", "w1", "w2")
COLS = ("bk", "bv", "bq", "lnq_g", "lnq_b", "lnm_g", "lnm_b", "b1")
ROWS = ("lnkv_g", "lnkv_b", "lnp_g", "lnp_b", "bu", "b2", "q_mu", "q_logsig", "cond0", "cond1")


class Lane:

    def __init__(self, engine, sem):
        self.engine, self.sem, self.count, self.seen = engine, sem, 0, {}

    def after(self, *marks):
        for sem, value in marks:
            if self.seen.get(sem.name, 0) < value:
                self.engine.wait_ge(sem, value)
                self.seen[sem.name] = value

    def did(self, instruction):
        instruction.then_inc(self.sem, 1)
        self.count += 1
        return self.sem, self.count


def build(nc, x, ctx_in, rows_in, bias_in, cols_in, mats_in, gate_wT, experts, out, scratch):
    stack = ExitStack()
    with stack:
        def sb(name, shape, dt=F32):
            return stack.enter_context(nc.sbuf_tensor(name, shape, dt))

        def sem(name):
            return stack.enter_context(nc.semaphore(name))

        pe = Lane(nc.tensor, sem("pe_done"))
        act = Lane(nc.scalar, sem("act_done"))
        dve = Lane(nc.vector, sem("dve_done"))
        pool = Lane(nc.gpsimd, sem("pool_done"))
        sync = Lane(nc.sync, sem("sync_unused"))

        xs = sb("xs", [P, B * T, D])
        slots = sb("slots", [P, B * T, D])
        mid = sb("mid", [P, B * T, D])
        hat = sb("hat", [P, B * T, D])
        hatT = [sb(f"hatT{b}", [P, DC, S]) for b in range(B)]
        attn = [sb(f"attn{b}", [P, 2, S]) for b in range(B)]
        gel = [sb(f"gel{b}", [P, DC, S]) for b in range(B)]
        ident = sb("ident", [P, P])
        mats = sb("mats", [P, len(MATS), DC, D])
        w1g = sb("w1g", [P, DC, D])
        rows = sb("rows", [P, len(ROWS), D])
        cols = sb("cols", [P, len(COLS), DC])
        expls = sb("expls", [P, D])

        def part(buffer, at, *dims):
            n = 1
            for d in dims:
                n *= d
            flat = buffer.rearrange("p a b -> p (a b)")[:, at:at + n]
            if len(dims) == 2:
                return flat.rearrange("p (a b) -> p a b", a=dims[0])
            return flat

        ctx = part(gel[1][0:NH, :, :], 0, J, D)
        ctxT = part(gel[1][:, :, :], J * D, DC, J * NH)
        kT, vT, kq_raw = (part(gel[0][:, :, :], i * DC * J * NH, DC, J * NH) for i in range(3))
        kq = sb("kq", [P, DC, J * NH])
        qk_bias = sb("qk_bias", [NH, J])
        b1g = sb("b1g", [P, DC])
        values = sb("values", [NH, J, VW])
        vscaled = [sb(f"vscaled{b}", [P, 2, VW]) for b in range(B)]
        eps_ones = sb("eps_ones", [NH, P])
        ROWSETS = B * T + J
        stat = sb("stat", [P, ROWSETS, 6])
        mv = sb("mv", [P, ROWSETS, 2])
        var_eps = sb("var_eps", [P, ROWSETS])
        rstd = sb("rstd", [P, ROWSETS])
        minus_half = sb("minus_half", [P, ROWSETS])
        neg_mean = sb("neg_mean", [P, ROWSETS])
        shift = sb("shift", [P, ROWSETS])
        rowmax = sb("rowmax", [NH, J, Q])
        shifted = sb("shifted", [NH, J])
        expbias = sb("expbias", [NH, J])
        rowsum = sb("rowsum", [NH, J, Q])
        rowtotal = sb("rowtotal", [NH, J])
        rrow = sb("rrow", [NH, J])
        rden = sb("rden", [P, B * T])
        gwT = sb("gwT", [P, DC, E])
        gbias = sb("gbias", [P, E])
        hatT_hi = [sb(f"hatT_hi{b}", [P, DC, S], F32R) for b in range(B)]
        hatT_lo = [sb(f"hatT_lo{b}", [P, DC, S], F32R) for b in range(B)]
        w_hi = [sb(f"w_hi{i}", [P, WCOL], F32R) for i in range(2)]
        w_lo = [sb(f"w_lo{i}", [P, WCOL], F32R) for i in range(2)]
        silu = [part(hat[:, :, :], i * BANK, BANK) for i in range(2)]
        act_in = [part(hat[:, :, :], (2 + i) * BANK, BANK) for i in range(2)]
        act_hi = [sb(f"act_hi{i}", [P, BANK], F32R) for i in range(2)]
        act_lo = [sb(f"act_lo{i}", [P, BANK], F32R) for i in range(2)]
        score, biased, masked, chosen, combine = (part(mats[:, i, :, :], 0, B * T, E) for i in range(5))
        pair_hi = sb("pair_hi", [P, TQ, EG, 2])
        pair_lo = sb("pair_lo", [P, TQ, EG, 2])
        gtop = sb("gtop", [P, TQ, EG])
        gsec = sb("gsec", [P, TQ, EG])
        gscore = sb("gscore", [P, TQ, EG + TOPG])
        gbest = sb("gbest", [P, TQ, 8])
        gleft = sb("gleft", [P, TQ, EG + TOPG])
        gmask = sb("gmask", [P, TQ, EG])
        ebest = sb("ebest", [P, TQ, 8])
        wsum = sb("wsum", [P, TQ])
        wnorm = sb("wnorm", [P, TQ])
        RAW = 4
        raw = [part(mid[:, :, :], i * WCOL, WCOL) for i in range(RAW)]

        ps = stack.enter_context(nc.psum_tensor("ps", [P, 8 * BANK], F32))
        bank_read = [None] * 8

        def bank(i, n=1):
            return ps[:, i * BANK:(i + n) * BANK]

        def mat(name, c):
            return mats[:, MATS.index(name), c, :]

        def row(name, p=P):
            return rows[0:p, ROWS.index(name), :]

        def col(name, c):
            i = COLS.index(name)
            return cols[:, i, c:c + 1]

        def pe_bank(i):
            if bank_read[i] is not None:
                pe.after(bank_read[i])

        def load(eng, name, dst, src):
            s = sem(name)
            eng.dma_start(dst, src).then_inc(s, 16)
            return s, 16

        ctx_in_sb = load(nc.sync, "ld_ctx", ctx[:, :, :], ctx_in.rearrange("b (h n) d -> n (b h) d", h=2))
        mats_in_sb = load(nc.sync, "ld_mats", mats[:, 0:4, :, :], mats_in[:, 0:4, :, :])
        x_in_sb = []
        for b in range(B):
            x_in_sb.append(load(nc.sync, f"ld_x{b}", xs[:, b * T:(b + 1) * T, :],
                                x[b].rearrange("(t p) d -> p t d", p=P)))
        mats2_in_sb = load(nc.sync, "ld_mats2", mats[:, 4:6, :, :], mats_in[:, 4:6, :, :])
        gwT_in_sb = load(nc.sync, "ld_gw", gwT[:, :, :], gate_wT)
        rows_in_sb = load(nc.scalar, "ld_rows", rows[:, :, :].rearrange("p r d -> p (r d)"),
                          rows_in.to_broadcast([P, len(ROWS) * D]))
        cols_in_sb = load(nc.scalar, "ld_cols", cols[:, :, :], cols_in)
        gbias_in_sb = load(nc.scalar, "ld_gb", gbias[:, :], bias_in.to_broadcast([P, E]))

        ident0 = pool.did(nc.gpsimd.memset(ident[:, :], 0.0))
        pool.after(ident0)
        identity = pool.did(nc.gpsimd.affine_select(
            out=ident[:, :], in_=ident[:, :], compare_op=ALU.not_equal, fill=1.0, base=0,
            pattern=[[-1, P]], channel_multiplier=1))
        half_set = pool.did(nc.gpsimd.memset(minus_half[:, :], -0.5))
        for b in range(B):
            pool.did(nc.gpsimd.memset(vscaled[b][:, :, :], 0.0))
            pool.did(nc.gpsimd.memset(attn[b][:, 0, :], 1.0))
        pool_constants = (pool.sem, pool.count)
        dve.did(nc.vector.memset(eps_ones[:, :], ATTN_EPS))
        constants = dve.did(nc.vector.memset(values[:, :, D:VW], 1.0))

        def norm_moments(tiles, source, parts=P):
            for g in tiles:
                last = dve.did(nc.vector.bn_stats(stat[0:parts, g, :], source(g)))
            dve.after(last)
            for g in tiles:
                last = dve.did(nc.vector.bn_aggr(mv[0:parts, g, :], stat[0:parts, g, :]))
            dve.after(last)
            a, z = tiles[0], tiles[-1] + 1
            dve.did(nc.vector.tensor_scalar_add(var_eps[0:parts, a:z], mv[0:parts, a:z, 1], LN_EPS))
            return dve.did(nc.vector.tensor_scalar(neg_mean[0:parts, a:z], mv[0:parts, a:z, 0], -1.0, None,
                                                   ALU.mult))

        def norm_rstd(tiles, moments, parts=P):
            a, z = tiles[0], tiles[-1] + 1
            pool.after(moments, half_set)
            return pool.did(nc.gpsimd.tensor_tensor(rstd[0:parts, a:z], var_eps[0:parts, a:z],
                                                    minus_half[0:parts, a:z], ALU.pow))

        def norm_stats(tiles, source, parts=P):
            return norm_rstd(tiles, norm_moments(tiles, source, parts), parts)

        def norm_apply(tiles, source, dest, scaled, parts=P):
            dve.after(scaled)
            return [dve.did(nc.vector.tensor_scalar(dest(g), source(g), mv[0:parts, g, 0:1],
                                                    rstd[0:parts, g:g + 1], ALU.subtract, ALU.mult))
                    for g in tiles]

        def norm_affine(tiles, source, dest, scaled, gain, shift):
            dve.after(scaled)
            marks = [dve.did(nc.vector.scalar_tensor_tensor(
                out=dest(g), in0=source(g), scalar=mv[:, g, 0:1], in1=gain,
                op0=ALU.subtract, op1=ALU.mult)) for g in tiles]
            last = None
            for g, m in zip(tiles, marks):
                dve.after(m)
                last = dve.did(nc.vector.scalar_tensor_tensor(
                    out=dest(g), in0=dest(g), scalar=rstd[:, g:g + 1], in1=shift,
                    op0=ALU.mult, op1=ALU.add))
            return last

        def transpose_block(b, q, source, ready, banks):
            marks = []
            for dc in range(DC):
                pe_bank(banks[dc])
            for i in range(TQ):
                g = b * T + q * TQ + i
                pe.after(ready[i])
                for dc in range(DC):
                    last = nc.tensor.transpose(bank(banks[dc])[:, i * P:(i + 1) * P],
                                               source(g)[:, dc * P:(dc + 1) * P], ident[:, :])
                    if i == TQ - 1:
                        marks.append(pe.did(last))
            return marks

        def interleave(streams, start):
            free = {"pe": 0.0, "act": 0.0, "dve": 0.0, "pool": 0.0}
            clock, done = list(start), {}
            upcoming = [next(s, None) for s in streams]
            while any(upcoming):
                starts = []
                for i, step in enumerate(upcoming):
                    if step and all(k in done for k in step[3]):
                        at = max([clock[i], *(done[k] for k in step[3])])
                        starts.append((max(at, free[step[0]]), at, i))
                at, _, i = min(starts)
                engine, took, key, _ = upcoming[i]
                free[engine] = at + took
                clock[i] = at + took + HANDOVER_US
                done[key] = clock[i]
                upcoming[i] = next(streams[i], None)

        made = {}

        def context():
            yield "dve", 2.0, None, ()
            dve.after(ctx_in_sb)
            halves = list(range(B * T, ROWSETS))
            piece = lambda g: ctx[:, g - B * T, :]
            moments = norm_moments(halves, piece, NH)
            yield "pool", 1.2, None, ()
            scaled = norm_rstd(halves, moments, NH)
            yield "dve", 3.6, None, ()
            last = norm_apply(halves, piece, piece, scaled, NH)
            dve.after(rows_in_sb, *last)
            last = [dve.did(nc.vector.tensor_tensor(ctx[:, j, :], ctx[:, j, :], row("lnkv_g", NH), ALU.mult))
                    for j in range(J)]
            ready = []
            for j in range(J):
                dve.after(last[j])
                ready.append(dve.did(nc.vector.tensor_tensor(ctx[:, j, :], ctx[:, j, :], row("lnkv_b", NH),
                                                             ALU.add)))
            yield "pe", 1.0, None, ()
            pe.after(identity)
            transposed = []
            for dc in range(DC):
                for j in range(J):
                    pe.after(ready[j])
                    last = nc.tensor.transpose(bank(4 + dc)[:, j * NH:(j + 1) * NH],
                                               ctx[:, j, dc * P:(dc + 1) * P], ident[0:NH, 0:NH])
                transposed.append(pe.did(last))
            yield "act", 1.0, None, ()
            for dc in range(DC):
                act.after(transposed[dc])
                ctxT_ready = bank_read[4 + dc] = act.did(nc.scalar.copy(ctxT[:, dc, :],
                                                                        bank(4 + dc)[:, 0:J * NH]))

            def project(bank0, weights, moving, n=J * NH):
                marks = []
                for oc in range(DC):
                    pe_bank(bank0 + oc)
                    for ic in range(DC):
                        last = nc.tensor.matmul(bank(bank0 + oc)[:, 0:n], weights(ic)[:, oc * P:(oc + 1) * P],
                                                moving(ic), start=ic == 0, stop=ic == DC - 1)
                    marks.append(pe.did(last))
                return marks

            yield "pe", 4.2, None, ()
            pe.after(ctxT_ready, mats_in_sb)
            k_sum = project(6, lambda c: mat("wk", c), lambda c: ctxT[:, c, :])
            v_sum = project(4, lambda c: mat("wv", c), lambda c: ctxT[:, c, :])
            yield "act", 2.2, None, ()
            act.after(cols_in_sb)
            for dest, sums, i, name in ((kT, k_sum, 6, "bk"), (vT, v_sum, 4, "bv")):
                for oc in range(DC):
                    act.after(sums[oc])
                    made[name] = bank_read[i + oc] = act.did(nc.scalar.activation(
                        dest[:, oc, :], bank(i + oc)[:, 0:J * NH], ACT.Identity, bias=col(name, oc)))
            yield "pe", 2.1, None, ()
            pe.after(made["bk"])
            kq_sum = project(6, lambda c: mat("wqT", c), lambda c: kT[:, c, :])
            yield "dve", 1.8, "kq", ()
            dve.after(cols_in_sb)
            for dc in range(DC):
                dve.after(kq_sum[dc])
                dve.did(nc.vector.tensor_scalar(kq[:, dc, :], bank(6 + dc)[:, 0:J * NH], col("lnq_g", dc), None,
                                                ALU.mult))
                made["kq"] = bank_read[6 + dc] = dve.did(nc.vector.tensor_copy(
                    kq_raw[:, dc, :], bank(6 + dc)[:, 0:J * NH]))
            yield "pe", 0.5, None, ()
            pe.after(made["kq"], cols_in_sb)
            pe_bank(6)
            for j in range(J):
                pairs = [(kq_raw, "lnq_b", c) for c in range(DC)] + [(kT, "bq", c) for c in range(DC)]
                for i, (left, name, c) in enumerate(pairs):
                    last = nc.tensor.matmul(bank(6)[0:NH, j:j + 1], left[:, c, j * NH:(j + 1) * NH], col(name, c),
                                            start=i == 0, stop=i == len(pairs) - 1)
            last = pe.did(last)
            yield "dve", 0.2, "qk_bias", ()
            dve.after(last)
            made["qk_bias"] = bank_read[6] = dve.did(nc.vector.tensor_copy(qk_bias[:, :], bank(6)[0:NH, 0:J]))
            for j in range(J):
                i = 4 + j % 2
                yield "pe", 0.9, None, ()
                pe.after(made["bv"], constants)
                pe_bank(i)
                for dc in range(DC):
                    last = nc.tensor.matmul(bank(i)[0:NH, 0:D], vT[:, dc, j * NH:(j + 1) * NH], mat("wu", dc),
                                            start=dc == 0, stop=dc == DC - 1)
                last = pe.did(last)
                yield "dve", 0.5, None, ()
                dve.after(last)
                made["values"] = bank_read[i] = dve.did(nc.vector.tensor_tensor(
                    values[:, j, 0:D], bank(i)[0:NH, 0:D], row("bu", NH), ALU.add))
            yield "pe", 1.8, None, ()
            pe.after(made["values"])
            sums = []
            for b in range(B):
                pe_bank(4 + b)
                for h in range(2):
                    last = nc.tensor.matmul(bank(4 + b)[:, 0:D + 1], eps_ones[:, :], values[:, 2 * b + h, 0:D + 1],
                                            start=h == 0, stop=h == 1)
                sums.append(pe.did(last))
            yield "dve", 0.6, "values", ()
            dve.after(pool_constants)
            for b in range(B):
                dve.after(sums[b])
                made["eps_row"] = bank_read[4 + b] = dve.did(nc.vector.tensor_copy(
                    vscaled[b][EPS_ROW:EPS_ROW + 1, 0, 0:D + 1], bank(4 + b)[EPS_ROW:EPS_ROW + 1, 0:D + 1]))
            yield "dve", 0.6, None, ()
            dve.after(mats2_in_sb)
            for dc in range(DC):
                made["w1g"] = dve.did(nc.vector.tensor_scalar(w1g[:, dc, :], mat("w1", dc), col("lnm_g", dc), None,
                                                              ALU.mult))
            yield "pe", 0.3, None, ()
            pe.after(mats2_in_sb)
            pe_bank(7)
            for fc in range(DC):
                for dc in range(DC):
                    last = nc.tensor.matmul(bank(7)[:, fc:fc + 1], mat("w1", dc)[:, fc * P:(fc + 1) * P],
                                            col("lnm_b", dc), start=dc == 0, stop=dc == DC - 1)
            last = pe.did(last)
            yield "dve", 1.0, "context", ()
            dve.after(last)
            made["b1g"] = bank_read[7] = dve.did(nc.vector.tensor_tensor(
                b1g[:, :], bank(7)[:, 0:DC], cols[:, COLS.index("b1"), :], ALU.add))
            for b in range(B):
                made["cond"] = dve.did(nc.vector.tensor_tensor(row(f"cond{b}"), row(f"cond{b}"), row("b2"),
                                                               ALU.add))

        act.after(rows_in_sb)
        expls_ready = act.did(nc.scalar.activation(expls[:, :], row("q_logsig"), ACT.Exp))

        max_ready = [[[None] * Q for _ in range(2)] for _ in range(B)]
        expbias_ready = [[None] * 2 for _ in range(B)]
        exp_done = [[None] * Q for _ in range(B)]
        vscaled_ready = [None] * B

        def evacuate(b, q, marks, banks, dest):
            out_marks = []
            for dc in range(DC):
                act.after(marks[dc])
                m = bank_read[banks[dc]] = act.did(nc.scalar.copy(
                    dest[:, dc, q * BANK:(q + 1) * BANK], bank(banks[dc])))
                out_marks.append(m)
            return out_marks

        def shift_means(tiles, scaled):
            a, z = tiles[0], tiles[-1] + 1
            pool.after(scaled)
            return pool.did(nc.gpsimd.tensor_tensor(shift[:, a:z], neg_mean[:, a:z], rstd[:, a:z], ALU.mult))

        def act_apply(tiles, source, dest, shifted_ready):
            act.after(shifted_ready)
            return [act.did(nc.scalar.activation(dest(g), source(g), ACT.Identity, bias=shift[:, g:g + 1],
                                                 scale=rstd[:, g:g + 1])) for g in tiles]

        def block(b, q):
            tiles = [b * T + q * TQ + i for i in range(TQ)]
            banks = (4 * b + q, 4 * b + 2 + q)
            span = slice(q * BANK, (q + 1) * BANK)
            source = lambda g: slots[:, g, :]
            middle = lambda g: mid[:, g, :]
            hatted = lambda g: hat[:, g, :]
            initial = lambda g: xs[:, g, :]
            yield "dve", 2.0, None, ()
            dve.after(x_in_sb[b])
            stats = norm_moments(tiles, initial)
            yield "pool", 1.2, None, ()
            scaled = norm_rstd(tiles, stats)
            yield "dve", 3.2, None, ()
            dve.after(expls_ready)
            ready = norm_affine(tiles, initial, source, scaled, expls[:, :], row("q_mu"))
            for r in range(ROUNDS):
                yield "dve", 2.0, None, ()
                dve.after(ready)
                stats = norm_moments(tiles, source)
                yield "pool", 1.2, None, ()
                shifted_ready = shift_means(tiles, norm_rstd(tiles, stats))
                yield "act", 2.0, None, ()
                normed = act_apply(tiles, source, hatted, shifted_ready)
                yield "pe", 0.5, None, ["context"] if b else ()
                pe.after(identity)
                marks = transpose_block(b, q, hatted, normed, banks)
                yield "act", 1.0, None, ()
                hatT_ready = evacuate(b, q, marks, banks, hatT[b])
                yield "pe", 3.5, None, ["kq"]
                logits_ready = []
                pe.after(made["kq"])
                for h in range(2):
                    j = 2 * b + h
                    pe_bank(banks[h])
                    pe.after(*hatT_ready)
                    for dc in range(DC):
                        last = nc.tensor.matmul(bank(banks[h])[0:NH, :], kq[:, dc, j * NH:(j + 1) * NH],
                                                hatT[b][:, dc, span], start=dc == 0, stop=dc == DC - 1)
                    logits_ready.append(pe.did(last))
                yield "dve", 1.2, ("max", b, q, r), ()
                for h in range(2):
                    dve.after(logits_ready[h])
                    max_ready[b][h][q] = dve.did(nc.vector.reduce_max(
                        rowmax[:, 2 * b + h, q:q + 1], bank(banks[h])[0:NH, :], AX.X))
                if q == 0:
                    yield "dve", 0.6, ("bias", b, r), [("max", b, i, r) for i in range(Q)] + ["qk_bias"]
                    dve.after(made["qk_bias"])
                    for h in range(2):
                        j = 2 * b + h
                        dve.after(*max_ready[b][h])
                        m = dve.did(nc.vector.scalar_tensor_tensor(
                            out=shifted[:, j:j + 1], in0=rowmax[:, j, 0:1], scalar=rowmax[:, j, 1:2],
                            in1=qk_bias[:, j:j + 1], op0=ALU.max, op1=ALU.add))
                        dve.after(m)
                        expbias_ready[b][h] = dve.did(nc.vector.tensor_scalar(
                            expbias[:, j:j + 1], qk_bias[:, j:j + 1], shifted[:, j:j + 1], SHARPEN,
                            ALU.subtract, ALU.mult))
                yield "act", 1.6, ("exp", b, q, r), [("bias", b, r)]
                for h in range(2):
                    j = 2 * b + h
                    act.after(expbias_ready[b][h])
                    exp_done[b][q] = bank_read[banks[h]] = act.did(nc.scalar.activation(
                        attn[b][0:NH, h, span], bank(banks[h])[0:NH, :], ACT.Exp, bias=expbias[:, j:j + 1],
                        scale=SHARPEN, accum_out=rowsum[:, j, q:q + 1]))
                if q == 0:
                    yield "dve", 1.0, ("values", b, r), [("exp", b, i, r) for i in range(Q)] + ["values"]
                    dve.after(*exp_done[b])
                    js = slice(2 * b, 2 * b + 2)
                    m = dve.did(nc.vector.tensor_tensor(rowtotal[:, js], rowsum[:, js, 0], rowsum[:, js, 1], ALU.add))
                    dve.after(m)
                    m = dve.did(nc.vector.reciprocal(rrow[:, js], rowtotal[:, js]))
                    dve.after(m)
                    for h in range(2):
                        j = 2 * b + h
                        vscaled_ready[b] = dve.did(nc.vector.tensor_scalar(
                            vscaled[b][0:NH, h, :], values[:, j, :], rrow[:, j:j + 1], None, ALU.mult))
                for i in range(0, TQ, 2):
                    yield "pe", 1.8, None, [("values", b, r)]
                    pe.after(exp_done[b][q], vscaled_ready[b], made["eps_row"])
                    for k in range(2):
                        t = q * TQ + i + k
                        pe_bank(banks[k])
                        for h in range(2):
                            n = EPS_ROW + 1 if h == 0 else NH
                            last = nc.tensor.matmul(bank(banks[k])[:, 0:D + 1], attn[b][0:n, h, t * P:(t + 1) * P],
                                                    vscaled[b][0:n, h, 0:D + 1], start=h == 0, stop=h == 1)
                    attended = pe.did(last)
                    yield "dve", 1.1, None, ()
                    dve.after(attended)
                    for k in range(2):
                        g = tiles[i + k]
                        m = dve.did(nc.vector.reciprocal(rden[:, g:g + 1], bank(banks[k])[:, D:D + 1]))
                    dve.after(m)
                    for k in range(2):
                        g = tiles[i + k]
                        m = bank_read[banks[k]] = dve.did(nc.vector.scalar_tensor_tensor(
                            out=mid[:, g, :], in0=bank(banks[k])[:, 0:D], scalar=rden[:, g:g + 1],
                            in1=slots[:, g, :], op0=ALU.mult, op1=ALU.add))
                yield "dve", 2.0, None, ()
                dve.after(m)
                stats = norm_moments(tiles, middle)
                yield "pool", 1.2, None, ()
                shifted_ready = shift_means(tiles, norm_rstd(tiles, stats))
                yield "act", 2.0, None, ()
                normed = act_apply(tiles, middle, hatted, shifted_ready)
                yield "pe", 0.5, None, ["context"]
                marks = transpose_block(b, q, hatted, normed, banks)
                pool.after(normed[-1], made["cond"])
                conditioned = pool.did(nc.gpsimd.tensor_tensor(
                    mid[:, tiles[0]:tiles[0] + TQ, :], mid[:, tiles[0]:tiles[0] + TQ, :],
                    row(f"cond{b}").rearrange("p (o d) -> p o d", o=1).to_broadcast([P, TQ, D]), ALU.add))
                yield "act", 1.0, None, ()
                hatT_ready = evacuate(b, q, marks, banks, hatT[b])
                yield "pe", 3.5, None, ()
                hidden = []
                pe.after(made["w1g"])
                for fc in range(DC):
                    pe_bank(banks[fc])
                    pe.after(*hatT_ready)
                    for dc in range(DC):
                        last = nc.tensor.matmul(bank(banks[fc]), w1g[:, dc, fc * P:(fc + 1) * P],
                                                hatT[b][:, dc, span], start=dc == 0, stop=dc == DC - 1)
                    hidden.append(pe.did(last))
                yield "act", 1.4, None, ()
                act.after(made["b1g"])
                for fc in range(DC):
                    act.after(hidden[fc])
                    gelu_ready = bank_read[banks[fc]] = act.did(nc.scalar.activation(
                        gel[b][:, fc, span], bank(banks[fc]), ACT.Gelu, bias=b1g[:, fc:fc + 1]))
                yield "pe", 3.5, None, ()
                pe.after(gelu_ready)
                out_ready = []
                for i in range(2):
                    pe_bank(banks[i])
                    for k in range(2):
                        s = (q * TQ + 2 * i + k) * P
                        for fc in range(DC):
                            last = nc.tensor.matmul(bank(banks[i])[:, k * D:(k + 1) * D], gel[b][:, fc, s:s + P],
                                                    mat("w2", fc), start=fc == 0, stop=fc == DC - 1)
                    out_ready.append(pe.did(last))
                yield "dve", 1.4, None, ()
                dve.after(conditioned)
                for i in range(2):
                    g = tiles[2 * i]
                    dve.after(out_ready[i])
                    m = bank_read[banks[i]] = dve.did(nc.vector.tensor_tensor(
                        mid[:, g:g + 2, :], bank(banks[i]).rearrange("p (t d) -> p t d", t=2),
                        mid[:, g:g + 2, :], ALU.add))
                yield "dve", 2.0, None, ()
                dve.after(m)
                stats = norm_moments(tiles, middle)
                yield "pool", 1.0, None, ()
                scaled = norm_rstd(tiles, stats)
                yield "dve", 3.2, None, ()
                ready = norm_affine(tiles, middle, source, scaled, row("lnp_g"), row("lnp_b"))
            yield from route(b, q, tiles, banks, span, ready)

        x1T = attn
        split_ready = [[None] * Q for _ in range(B)]
        x1T_ready = [[None] * Q for _ in range(B)]
        hat_free, mid_free, gel_free = [], [], []
        weights_stored = [[None] * Q for _ in range(B)]
        sentinels = dve.did(nc.vector.memset(gscore[:, :, EG:], LOW))

        def route(b, q, tiles, banks, span, ready):
            hatted = lambda g: hat[:, g, :]
            summed = lambda g: xs[:, g, :]
            ts = slice(tiles[0], tiles[0] + TQ)
            mid_free.append(ready)
            gel_free.append(ready)
            yield "dve", 3.2, None, ()
            dve.after(ready)
            added = dve.did(nc.vector.tensor_tensor(xs[:, ts, :], xs[:, ts, :], slots[:, ts, :], ALU.add))
            dve.after(added)
            stats = norm_moments(tiles, summed)
            yield "pool", 1.2, None, ()
            shifted_ready = shift_means(tiles, norm_rstd(tiles, stats))
            yield "act", 2.0, None, ()
            normed = act_apply(tiles, summed, hatted, shifted_ready)
            yield "pe", 0.5, None, ()
            marks = transpose_block(b, q, hatted, normed, banks)
            hat_free.append(marks[-1])
            yield "act", 2.0, None, ()
            copied = []
            for dc in range(DC):
                act.after(marks[dc])
                act.did(nc.scalar.copy(hatT_hi[b][:, dc, span], bank(banks[dc])))
                m = bank_read[banks[dc]] = act.did(nc.scalar.copy(hatT[b][:, dc, span], bank(banks[dc])))
                copied.append(m)
            yield "pe", 1.6, None, ()
            pe.after(gwT_in_sb, *copied)
            pe_bank(banks[0])
            for i in range(TQ):
                for dc in range(DC):
                    s = (q * TQ + i) * P
                    last = nc.tensor.matmul(bank(banks[0])[:, i * E:(i + 1) * E], hatT[b][:, dc, s:s + P],
                                            gwT[:, dc, :], start=dc == 0, stop=dc == DC - 1)
            gate_ready = pe.did(last)
            yield "act", 1.5, None, ()
            act.after(gate_ready)
            scored = bank_read[banks[0]] = act.did(nc.scalar.activation(
                score[:, ts, :], bank(banks[0])[:, 0:TQ * E].rearrange("p (t e) -> p t e", e=E), ACT.Sigmoid))
            yield "dve", 6.0, None, ()
            dve.after(scored, gbias_in_sb, sentinels)

            def step(instruction):
                m = dve.did(instruction)
                dve.after(m)
                return m

            step(nc.vector.tensor_tensor(biased[:, ts, :], score[:, ts, :],
                                         gbias[:, :].rearrange("p (o e) -> p o e", o=1).to_broadcast([P, TQ, E]),
                                         ALU.add))
            four = biased[:, ts, :].rearrange("p t (g u v) -> p (t g) u v", g=EG, u=2)
            hi4 = pair_hi[:, :, :, :].rearrange("p t g u -> p (t g) u")
            lo4 = pair_lo[:, :, :, :].rearrange("p t g u -> p (t g) u")
            top, sec = (a[:, :, :].rearrange("p t g -> p (t g)") for a in (gtop, gsec))
            dve.did(nc.vector.tensor_tensor(hi4, four[:, :, :, 0], four[:, :, :, 1], ALU.max))
            step(nc.vector.tensor_tensor(lo4, four[:, :, :, 0], four[:, :, :, 1], ALU.min))
            dve.did(nc.vector.tensor_tensor(top, hi4[:, :, 0], hi4[:, :, 1], ALU.max))
            dve.did(nc.vector.tensor_tensor(sec, hi4[:, :, 0], hi4[:, :, 1], ALU.min))
            step(nc.vector.tensor_tensor(lo4[:, :, 0], lo4[:, :, 0], lo4[:, :, 1], ALU.max))
            step(nc.vector.tensor_tensor(sec, sec, lo4[:, :, 0], ALU.max))
            step(nc.vector.tensor_tensor(gscore[:, :, 0:EG], gtop[:, :, :], gsec[:, :, :], ALU.add))
            for i in range(TQ):
                m = dve.did(nc.vector.max(gbest[:, i, :], gscore[:, i, :]))
            dve.after(m)
            step(nc.vector.memset(gbest[:, :, TOPG:], LOW))
            for i in range(TQ):
                m = dve.did(nc.vector.match_replace(gleft[:, i, :], gbest[:, i, :], gscore[:, i, :], STRUCK))
            dve.after(m)
            step(nc.vector.tensor_tensor(gmask[:, :, :], gleft[:, :, 0:EG], gscore[:, :, 0:EG], ALU.not_equal))
            step(nc.vector.tensor_tensor(
                masked[:, ts, :].rearrange("p t (g v) -> p (t g) v", g=EG),
                biased[:, ts, :].rearrange("p t (g v) -> p (t g) v", g=EG),
                gmask[:, :, :].rearrange("p t (g o) -> p (t g) o", o=1).to_broadcast([P, TQ * EG, GE]), ALU.mult))
            for i in range(TQ):
                m = dve.did(nc.vector.max(ebest[:, i, :], masked[:, tiles[i], :]))
            dve.after(m)
            for i in range(TQ):
                m = dve.did(nc.vector.match_replace(chosen[:, tiles[i], :], ebest[:, i, :], masked[:, tiles[i], :],
                                                    STRUCK))
            dve.after(m)
            step(nc.vector.tensor_tensor(chosen[:, ts, :], chosen[:, ts, :], masked[:, ts, :], ALU.not_equal))
            step(nc.vector.tensor_tensor(chosen[:, ts, :], chosen[:, ts, :], score[:, ts, :], ALU.mult))
            step(nc.vector.reduce_sum(wsum[:, :], chosen[:, ts, :], AX.X))
            step(nc.vector.tensor_scalar_add(wsum[:, :], wsum[:, :], 1e-20))
            step(nc.vector.reciprocal(wnorm[:, :], wsum[:, :]))
            step(nc.vector.tensor_scalar(wnorm[:, :], wnorm[:, :], ROUTE_SCALE, None, ALU.mult))
            weighed = dve.did(nc.vector.tensor_tensor(
                combine[:, ts, :], chosen[:, ts, :],
                wnorm[:, :].rearrange("p (t o) -> p t o", o=1).to_broadcast([P, TQ, E]), ALU.mult))
            yield "pe", 0.5, None, ()
            pe.after(weighed)
            pe_bank(banks[1])
            for i in range(TQ):
                last = nc.tensor.transpose(bank(banks[1])[0:E, i * P:(i + 1) * P], combine[:, tiles[i], :],
                                           ident[:, :])
            turned = pe.did(last)
            yield "act", 0.7, None, ()
            act.after(turned, added)
            combT = part(slots[0:E, ts, :], 0, BANK)
            m = bank_read[banks[1]] = act.did(nc.scalar.copy(combT, bank(banks[1])[0:E, :]))
            sync.after(m)
            s = sem(f"st_comb{b}{q}")
            nc.sync.dma_start(scratch[b][:, span], combT).then_inc(s, 16)
            weights_stored[b][q] = (s, 16)
            yield "dve", 1.3, None, ()
            for dc in range(DC):
                dve.after(copied[dc])
                split_ready[b][q] = dve.did(nc.vector.tensor_tensor(
                    hatT_lo[b][:, dc, span], hatT[b][:, dc, span], hatT_hi[b][:, dc, span].bitcast(F32),
                    ALU.subtract))
            yield "pe", 0.5, None, ()
            marks = transpose_block(b, q, summed, [added] * TQ, banks)
            yield "act", 1.0, None, ()
            x1T_ready[b][q] = evacuate(b, q, marks, banks, x1T[b])

        interleave([context()] + [block(b, q) for b in range(B) for q in range(Q)],
                   [0] + [1 + BATCH_LAG_US * b + BLOCK_LAG_US * q for b in range(B) for q in range(Q)])

        CW = 4
        cweight = [gel[i // 2][:, i % 2, :] for i in range(CW)]
        raw_sem = [sem(f"ld_w{i}") for i in range(RAW)]
        cw_sem = [sem(f"ld_c{i}") for i in range(CW)]
        split_w = [None] * RAW
        cw_read = [None] * CW
        w_read = [None] * 2
        EXPERTS = E + SHARED
        order = [(b, e) for b in range(B) for e in range(EXPERTS)]
        w_count = c_count = 0
        w_loaded, c_loaded = {}, {}

        def load_expert(n):
            nonlocal w_count, c_count
            b, e = order[n]
            i = w_count % RAW
            sync.after(*(mid_free if split_w[i] is None else [split_w[i]]))
            nc.sync.dma_start(raw[i], experts[e]).then_inc(raw_sem[i], 16)
            w_loaded[n] = (i, (raw_sem[i], 16 * (w_count // RAW + 1)))
            w_count += 1
            if e < E:
                i = c_count % CW
                sync.after(*weights_stored[b], *(gel_free if cw_read[i] is None else [cw_read[i]]))
                nc.sync.dma_start(cweight[i], scratch[b, e:e + 1, :].to_broadcast([P, S])).then_inc(cw_sem[i], 16)
                c_loaded[n] = (i, (cw_sem[i], 16 * (c_count // CW + 1)))
                c_count += 1

        w_ready = {}

        def split_weights(n):
            i, loaded = w_loaded[n]
            act.after(loaded)
            if w_read[n % 2] is not None:
                act.after(w_read[n % 2])
            hi = act.did(nc.scalar.copy(w_hi[n % 2][:, :], raw[i]))
            dve.after(hi, loaded)
            w_ready[n] = split_w[i] = dve.did(nc.vector.tensor_tensor(
                w_lo[n % 2][:, :], raw[i], w_hi[n % 2][:, :].bitcast(F32), ALU.subtract))

        def three_passes(dest, left, right, first, final):
            terms = [(a, c) for (lh, ll), (rh, rl) in zip(left, right) for a, c in ((lh, rh), (lh, rl), (ll, rh))]
            for k, (a, c) in enumerate(terms):
                last = nc.tensor.matmul(dest, a, c, start=first and k == 0, stop=final and k == len(terms) - 1)
            return last

        act.after(*hat_free)
        dve.after(*hat_free)
        blocks = [(n, q) for n in range(len(order)) for q in range(Q)]
        up_done, gate_done, inner_ready = {}, {}, {}
        down_done = {}

        def gate_up(m):
            n, q = blocks[m]
            b, e = order[n]
            hi, lo = w_hi[n % 2], w_lo[n % 2]
            pe.after(w_ready[n], split_ready[b][q])
            span = slice(q * BANK, (q + 1) * BANK)
            for which, done in ((0, gate_done), (1, up_done)):
                i = 4 + 2 * (m % 2) + which
                pe_bank(i)
                o = [which * D + dc * P for dc in range(DC)]
                done[m] = pe.did(three_passes(
                    bank(i), [(hi[:, a:a + P], lo[:, a:a + P]) for a in o],
                    [(hatT_hi[b][:, dc, span], hatT_lo[b][:, dc, span]) for dc in range(DC)], True, True))

        def gated(m):
            n, q = blocks[m]
            b, e = order[n]
            u = m % 2
            act.after(gate_done[m])
            if m >= 2:
                act.after(inner_ready[m - 2])
            s = bank_read[4 + 2 * u] = act.did(nc.scalar.activation(silu[u][:, :], bank(4 + 2 * u), ACT.Silu))
            dve.after(s)
            if e < E:
                i, loaded = c_loaded[n]
                dve.after(loaded)
                cw_read[i] = dve.did(nc.vector.tensor_tensor(
                    silu[u][:, :], silu[u][:, :], cweight[i][:, q * BANK:(q + 1) * BANK], ALU.mult))
                dve.after(cw_read[i])
            dve.after(up_done[m])
            v = bank_read[5 + 2 * u] = dve.did(nc.vector.tensor_tensor(
                act_in[u][:, :], bank(5 + 2 * u), silu[u][:, :], ALU.mult))
            dve.after(v)
            if m >= 2:
                dve.after(down_done[m - 2])
            h = dve.did(nc.vector.tensor_copy(act_hi[u][:, :], act_in[u][:, :]))
            dve.after(h)
            inner_ready[m] = dve.did(nc.vector.tensor_tensor(
                act_lo[u][:, :], act_in[u][:, :], act_hi[u][:, :].bitcast(F32), ALU.subtract))

        def down(m):
            n, q = blocks[m]
            b, e = order[n]
            u = m % 2
            pe.after(inner_ready[m])
            for dc in range(DC):
                i = 2 * dc + q
                if e == 0:
                    pe_bank(i)
                a = 2 * D + dc * P
                last = three_passes(bank(i), [(w_hi[n % 2][:, a:a + P], w_lo[n % 2][:, a:a + P])],
                                    [(act_hi[u][:, :], act_lo[u][:, :])], e == 0, e == EXPERTS - 1)
            down_done[m] = pe.did(last)
            if q == Q - 1:
                w_read[n % 2] = down_done[m]
            if q == Q - 1 and e == EXPERTS - 1:
                finish(b)

        stored = []

        def finish(b):
            dve.after(*x1T_ready[b][0], *x1T_ready[b][1], down_done[Q * ((b + 1) * EXPERTS) - 1])
            for q in range(Q):
                for dc in range(DC):
                    span = slice(q * BANK, (q + 1) * BANK)
                    m = bank_read[2 * dc + q] = dve.did(nc.vector.tensor_tensor(
                        hatT[b][:, dc, span], bank(2 * dc + q), x1T[b][:, dc, span], ALU.add))
                sync.after(m)
                s = sem(f"st_out{b}{q}")
                nc.sync.dma_start(out[b, :, :, q * BANK:(q + 1) * BANK].rearrange("c p s -> p c s"),
                                  hatT[b][:, :, span]).then_inc(s, 16)
                stored.append((s, 16))

        AHEAD = 3
        for n in range(AHEAD):
            load_expert(n)
        split_weights(0)
        gate_up(0)
        for m in range(len(blocks)):
            n, q = blocks[m]
            if q == 0 and n + AHEAD < len(order):
                load_expert(n + AHEAD)
            gated(m)
            if q == 0 and n + 1 < len(order):
                split_weights(n + 1)
            if m + 1 < len(blocks):
                gate_up(m + 1)
            down(m)
        sync.after(*stored)


def kernel(**inputs):
    import numpy as np
    import concourse.bacc as bacc
    from concourse.bass_utils import run_bass_kernel_spmd

    a = {k.replace("L0_xcond_", "").replace("L0_ffn_", ""): np.asarray(v) for k, v in inputs.items()}
    chunked = lambda w: w.reshape(DC, P, -1).transpose(1, 0, 2)
    a["wqT"] = a["wq"].T
    a["cond0"], a["cond1"] = a["cond_1024"]
    mats = np.stack([chunked(a[n]) for n in MATS], axis=1)
    cols = np.stack([a[n].reshape(DC, P).T for n in COLS], axis=1)
    rows = np.concatenate([a[n].reshape(1, D) for n in ROWS], axis=1)

    def expert(gate, up, down):
        return np.concatenate([chunked(gate.T).reshape(P, D), chunked(up.T).reshape(P, D), down.T], axis=1)

    experts = np.stack(
        [expert(a["w_gate"][e], a["w_up"][e], a["w_down"][e]) for e in range(E)]
        + [expert(a["sh_gate"][s:s + I], a["sh_up"][s:s + I], a["sh_down"][:, s:s + I])
           for s in range(0, SHARED * I, I)])
    arrays = {
        "x": a["x"], "ctx": a["ctx_1024"], "rows": rows, "gate_bias": a["gate_bias"].reshape(1, E), "cols": cols,
        "mats": mats, "gate_wT": chunked(a["gate_w"].T), "experts": experts,
    }
    arrays = {k: np.ascontiguousarray(v) for k, v in arrays.items()}
    nc = bacc.Bacc("TRN2", target_bir_lowering=False, num_devices=1)
    args = [nc.dram_tensor(f"in_{n}", v.shape, F32, kind="ExternalInput").ap() for n, v in arrays.items()]
    out = nc.dram_tensor("out", (B, DC, P, S), F32, kind="ExternalOutput").ap()
    scratch = nc.dram_tensor("routing", (B, E, S), F32, kind="Internal").ap()
    build(nc, *args, out, scratch)
    got = run_bass_kernel_spmd(nc, [{f"in_{n}": v for n, v in arrays.items()}], core_ids=[0]).results[0]["out"]
    return np.ascontiguousarray(got.reshape(B, D, S).transpose(0, 2, 1))
```

```python
from contextlib import ExitStack

import concourse.bass as bass
from concourse import mybir

F32 = mybir.dt.float32
F32R = mybir.dt.float32r
ALU = mybir.AluOpType
ACT = mybir.ActivationFunctionType
AX = mybir.AxisListType

P = 128
BANK = 512
D = 256
DC = D // P
B = 2
S = 1024
T = S // P
Q = S // BANK
TQ = T // Q
N_CTX = 154
NH = N_CTX // 2
J = 2 * B
ROUNDS = 3
TABLE_LOAD_US = 1.3
HANDOVER_US = 0.2
BLOCK_START_US = ((6, 9), (16, 19))
BLOCK_HANDICAP_US = ((0, 0), (0.3, 0.5))
EXPERT_HANDICAP_US = (0, 0.3, 0.1, 0)
SHARPEN = float(D) ** 0.5
LN_EPS = 1e-5
ATTN_EPS = 1e-8
EPS_ROW = 96
VW = D + 2

E = 32
I = 128
SHARED = 2
EG = 8
GE = E // EG
TOPG = 4
TOPK = 8
ROUTE_SCALE = 2.5
LOW = -3.0e38
STRUCK = -2.0e38
WCOL = 3 * D

MATS = ("wk", "wv", "wqT", "wu", "w1", "w2")
COLS = ("lnkv_g", "lnkv_b", "bk", "bv", "bq", "lnq_g", "lnq_b", "lnm_g", "lnm_b", "b1")
ROWS = ("q_mu", "q_logsig", "bu", "b2", "cond0", "cond1", "lnp_g", "lnp_b")


class Lane:

    def __init__(self, engine, sem):
        self.engine, self.sem, self.count, self.seen = engine, sem, 0, {}

    def after(self, *marks):
        for sem, value in marks:
            if self.seen.get(sem.name, 0) < value:
                self.engine.wait_ge(sem, value)
                self.seen[sem.name] = value

    def did(self, instruction):
        instruction.then_inc(self.sem, 1)
        self.count += 1
        return self.sem, self.count


def build(nc, x, ctx_in, rows_in, bias_in, cols_in, mats_in, gate_wT, experts, out, scratch):
    stack = ExitStack()
    with stack:
        def sb(name, shape, dt=F32):
            return stack.enter_context(nc.sbuf_tensor(name, shape, dt))

        def sem(name):
            return stack.enter_context(nc.semaphore(name))

        pe = Lane(nc.tensor, sem("pe_done"))
        act = Lane(nc.scalar, sem("act_done"))
        dve = Lane(nc.vector, sem("dve_done"))
        pool = Lane(nc.gpsimd, sem("pool_done"))
        sync = Lane(nc.sync, None)

        xs = sb("xs", [P, B * T, D])
        slots = sb("slots", [P, B * T, D])
        mid = sb("mid", [P, B * T, D])
        hat = sb("hat", [P, B * T, D])
        hatT = [sb(f"hatT{b}", [P, DC, S]) for b in range(B)]
        attn = [sb(f"attn{b}", [P, 2, S]) for b in range(B)]
        gel = [sb(f"gel{b}", [P, DC, S]) for b in range(B)]
        ident = sb("ident", [P, P])
        mats = sb("mats", [P, len(MATS), DC, D])
        w1g = sb("w1g", [P, DC, D])
        rows = sb("rows", [P, len(ROWS), D])
        cols = sb("cols", [P, len(COLS), DC])
        expls = sb("expls", [P, D])

        def part(buffer, at, *dims):
            n = 1
            for d in dims:
                n *= d
            flat = buffer.rearrange("p a b -> p (a b)")[:, at:at + n]
            if len(dims) == 2:
                return flat.rearrange("p (a b) -> p a b", a=dims[0])
            return flat

        ctx = part(gel[1][0:NH, :, :], 0, J, D)
        ctxT = part(gel[1][:, :, :], J * D, DC, J * NH)
        kT, vT, kq_raw = (part(gel[0][:, :, :], i * DC * J * NH, DC, J * NH) for i in range(3))
        kq = sb("kq", [P, DC, J * NH])
        qk_bias = sb("qk_bias", [NH, J])
        b1g = sb("b1g", [P, DC])
        values = sb("values", [NH, J, VW])
        vscaled = [sb(f"vscaled{b}", [P, 2, VW]) for b in range(B)]
        eps_ones = sb("eps_ones", [NH, P])
        ROWSETS = B * T + J
        stat = sb("stat", [P, ROWSETS, 6])
        mv = sb("mv", [P, ROWSETS, 2])
        var_eps = sb("var_eps", [P, ROWSETS])
        rstd = sb("rstd", [P, ROWSETS])
        minus_half = sb("minus_half", [P, ROWSETS])
        total = sb("total", [P, B * T])
        variance = sb("variance", [P, B * T])
        neg_mean_scaled = sb("neg_mean_scaled", [P, B * T])
        neg_mean = sb("neg_mean", [P, ROWSETS])
        shift = sb("shift", [P, ROWSETS])
        rowmax = sb("rowmax", [NH, J, Q])
        shifted = sb("shifted", [NH, J])
        expbias = sb("expbias", [NH, J])
        rowsum = sb("rowsum", [NH, J, Q])
        rowtotal = sb("rowtotal", [NH, J])
        rrow = sb("rrow", [NH, J])
        rden = sb("rden", [P, B * T])
        gwT = sb("gwT", [P, DC, E])
        gbias = sb("gbias", [P, E])
        hatT_hi = [sb(f"hatT_hi{b}", [P, DC, S], F32R) for b in range(B)]
        hatT_lo = [sb(f"hatT_lo{b}", [P, DC, S], F32R) for b in range(B)]
        w_hi = [sb(f"w_hi{i}", [P, WCOL], F32R) for i in range(2)]
        w_lo = [sb(f"w_lo{i}", [P, WCOL], F32R) for i in range(2)]
        silu = [part(hat[:, :, :], i * BANK, BANK) for i in range(2)]
        act_in = [part(hat[:, :, :], (2 + i) * BANK, BANK) for i in range(2)]
        act_hi = [sb(f"act_hi{i}", [P, BANK], F32R) for i in range(2)]
        act_lo = [sb(f"act_lo{i}", [P, BANK], F32R) for i in range(2)]
        score, biased, masked, chosen, combine = (part(mats[:, i, :, :], 0, B * T, E) for i in range(5))
        pair_hi = [sb(f"pair_hi{q}", [P, TQ, EG, 2]) for q in range(Q)]
        pair_lo = [sb(f"pair_lo{q}", [P, TQ, EG, 2]) for q in range(Q)]
        gtop = [sb(f"gtop{q}", [P, TQ, EG]) for q in range(Q)]
        gsec = [sb(f"gsec{q}", [P, TQ, EG]) for q in range(Q)]
        gscore = [sb(f"gscore{q}", [P, TQ, EG + TOPG]) for q in range(Q)]
        gbest = [sb(f"gbest{q}", [P, TQ, 8]) for q in range(Q)]
        gleft = [sb(f"gleft{q}", [P, TQ, EG + TOPG]) for q in range(Q)]
        gmask = [sb(f"gmask{q}", [P, TQ, EG]) for q in range(Q)]
        ebest = [sb(f"ebest{q}", [P, TQ, 8]) for q in range(Q)]
        wsum = [sb(f"wsum{q}", [P, TQ]) for q in range(Q)]
        wnorm = [sb(f"wnorm{q}", [P, TQ]) for q in range(Q)]

        ps = stack.enter_context(nc.psum_tensor("ps", [P, 8 * BANK], F32))
        bank_read = [None] * 8

        def bank(i, n=1):
            return ps[:, i * BANK:(i + n) * BANK]

        def mat(name, c):
            return mats[:, MATS.index(name), c, :]

        def row(name, p=P):
            return rows[0:p, ROWS.index(name), :]

        def col(name, c):
            i = COLS.index(name)
            return cols[:, i, c:c + 1]

        def pe_bank(i):
            if bank_read[i] is not None:
                pe.after(bank_read[i])

        def load(eng, name, dst, src):
            s = sem(name)
            eng.dma_start(dst, src).then_inc(s, 16)
            return s, 16

        mats_in_sb, x_in_sb = {}, {}

        def load_mat(name):
            i = MATS.index(name)
            mats_in_sb[name] = load(nc.sync, f"ld_mat_{name}", mats[:, i, :, :], mats_in[:, i, :, :])

        def load_x(b, q):
            t = b * T + q * TQ
            x_in_sb[b, q] = load(nc.sync, f"ld_x{b}{q}", xs[:, t:t + TQ, :],
                                 x[b, q * BANK:(q + 1) * BANK, :].rearrange("(t p) d -> p t d", p=P))

        def load_rows(name, a, z):
            return load(nc.scalar, name, rows[:, a:z, :].rearrange("p r d -> p (r d)"),
                        rows_in[:, a * D:z * D].to_broadcast([P, (z - a) * D]))

        ctx_in_sb = load(nc.sync, "ld_ctx", ctx[:, :, :], ctx_in.rearrange("b (h n) d -> n (b h) d", h=2))
        cols_in_sb = load(nc.scalar, "ld_cols", cols[:, :, :], cols_in)
        first_rows_in_sb = load_rows("ld_rows_q", 0, 2)
        load_x(0, 0)
        load_mat("wk")
        load_mat("wqT")
        load_x(0, 1)
        load_mat("wv")
        load_mat("wu")
        rows_in_sb = load_rows("ld_rows", 2, len(ROWS))
        load_x(1, 0)
        load_mat("w1")
        load_mat("w2")
        load_x(1, 1)
        gwT_in_sb = load(nc.sync, "ld_gw", gwT[:, :, :], gate_wT)
        gbias_in_sb = load(nc.scalar, "ld_gb", gbias[:, :], bias_in.to_broadcast([P, E]))

        ident0 = pool.did(nc.gpsimd.memset(ident[:, :], 0.0))
        pool.after(ident0)
        identity = pool.did(nc.gpsimd.affine_select(
            out=ident[:, :], in_=ident[:, :], compare_op=ALU.not_equal, fill=1.0, base=0,
            pattern=[[-1, P]], channel_multiplier=1))
        half_set = pool.did(nc.gpsimd.memset(minus_half[:, :], -0.5))
        for b in range(B):
            pool.did(nc.gpsimd.memset(vscaled[b][:, :, :], 0.0))
            pool.did(nc.gpsimd.memset(attn[b][:, 0, :], 1.0))
        pool_constants = (pool.sem, pool.count)
        dve.did(nc.vector.memset(eps_ones[:, :], ATTN_EPS))
        constants = dve.did(nc.vector.memset(values[:, :, D:VW], 1.0))

        def norm_moments(tiles, source, parts=P):
            for g in tiles:
                last = dve.did(nc.vector.bn_stats(stat[0:parts, g, :], source(g)))
            dve.after(last)
            for g in tiles:
                last = dve.did(nc.vector.bn_aggr(mv[0:parts, g, :], stat[0:parts, g, :]))
            dve.after(last)
            a, z = tiles[0], tiles[-1] + 1
            dve.did(nc.vector.tensor_scalar_add(var_eps[0:parts, a:z], mv[0:parts, a:z, 1], LN_EPS))
            return dve.did(nc.vector.tensor_scalar(neg_mean[0:parts, a:z], mv[0:parts, a:z, 0], -1.0, None,
                                                   ALU.mult))

        def norm_rstd(tiles, moments, parts=P):
            a, z = tiles[0], tiles[-1] + 1
            pool.after(moments, half_set)
            return pool.did(nc.gpsimd.tensor_tensor(rstd[0:parts, a:z], var_eps[0:parts, a:z],
                                                    minus_half[0:parts, a:z], ALU.pow))

        def norm_apply(tiles, source, dest, scaled, parts=P):
            dve.after(scaled)
            return [dve.did(nc.vector.tensor_scalar(dest(g), source(g), mv[0:parts, g, 0:1],
                                                    rstd[0:parts, g:g + 1], ALU.subtract, ALU.mult))
                    for g in tiles]

        def norm_affine(tiles, source, dest, scaled, gain, shift):
            dve.after(scaled)
            marks = [dve.did(nc.vector.scalar_tensor_tensor(
                out=dest(g), in0=source(g), scalar=mv[:, g, 0:1], in1=gain,
                op0=ALU.subtract, op1=ALU.mult)) for g in tiles]
            for g, m in zip(tiles, marks):
                dve.after(m)
                last = dve.did(nc.vector.scalar_tensor_tensor(
                    out=dest(g), in0=dest(g), scalar=rstd[:, g:g + 1], in1=shift,
                    op0=ALU.mult, op1=ALU.add, accum_out=total[:, g:g + 1]))
            return negative_means(tiles, last)

        def negative_means(tiles, totals_ready):
            a, z = tiles[0], tiles[-1] + 1
            dve.after(totals_ready)
            dve.did(nc.vector.tensor_scalar(neg_mean[:, a:z], total[:, a:z], -1.0 / D, None, ALU.mult))
            return dve.did(nc.vector.tensor_scalar(neg_mean_scaled[:, a:z], total[:, a:z], -D ** -1.5, None,
                                                   ALU.mult))

        def variances(tiles, source, ready):
            act.after(ready)
            for g in tiles:
                last = act.did(nc.scalar.activation(hat[:, g, :], source(g), ACT.Square,
                                                    bias=neg_mean_scaled[:, g:g + 1], scale=D ** -0.5,
                                                    accum_out=variance[:, g:g + 1]))
            return last

        def rstd_and_shift(tiles, ready):
            a, z = tiles[0], tiles[-1] + 1
            pool.after(ready)
            m = pool.did(nc.gpsimd.tensor_scalar(var_eps[:, a:z], variance[:, a:z], LN_EPS, None, ALU.add))
            return shift_means(tiles, norm_rstd(tiles, m))

        def transpose_block(b, q, source, ready, banks):
            marks = []
            for dc in range(DC):
                pe_bank(banks[dc])
            for i in range(TQ):
                g = b * T + q * TQ + i
                pe.after(ready[i])
                for dc in range(DC):
                    last = nc.tensor.transpose(bank(banks[dc])[:, i * P:(i + 1) * P],
                                               source(g)[:, dc * P:(dc + 1) * P], ident[:, :])
                    if i == TQ - 1:
                        marks.append(pe.did(last))
            return marks

        def interleave(streams):
            free = {"pe": 0.0, "act": 0.0, "dve": 0.0, "pool": 0.0}
            clock, done = [start for _, start, _ in streams], {}
            upcoming = [next(s, None) for s, _, _ in streams]
            loaded = None
            while any(upcoming):
                starts = []
                for i, step in enumerate(upcoming):
                    if step and all(k in done for k in step[3]):
                        engine, _, table = step[0].partition(" ")
                        at = max([clock[i], free[engine], *(done[k] for k in step[3])])
                        if table and table != loaded:
                            at += TABLE_LOAD_US
                        starts.append((at + streams[i][2], at, i))
                _, at, i = min(starts)
                kind, took, key, _ = upcoming[i]
                engine, _, table = kind.partition(" ")
                loaded = table or loaded
                free[engine] = at + took
                clock[i] = at + took + HANDOVER_US
                done[key] = clock[i]
                upcoming[i] = next(streams[i][0], None)

        made = {}

        def project(bank0, weights, moving, n=J * NH):
            marks = []
            for oc in range(DC):
                pe_bank(bank0 + oc)
                for ic in range(DC):
                    last = nc.tensor.matmul(bank(bank0 + oc)[:, 0:n], weights(ic)[:, oc * P:(oc + 1) * P],
                                            moving(ic), start=ic == 0, stop=ic == DC - 1)
                marks.append(pe.did(last))
            return marks

        def add_bias(dest, sums, bank0, name):
            for oc in range(DC):
                act.after(sums[oc])
                made[name] = bank_read[bank0 + oc] = act.did(nc.scalar.activation(
                    dest[:, oc, :], bank(bank0 + oc)[:, 0:J * NH], ACT.Identity, bias=col(name, oc)))

        def context_keys():
            yield "dve", 2.0, None, ()
            dve.after(ctx_in_sb)
            halves = list(range(B * T, ROWSETS))
            piece = lambda g: ctx[:, g - B * T, :]
            moments = norm_moments(halves, piece, NH)
            yield "pool", 1.0, None, ()
            scaled = norm_rstd(halves, moments, NH)
            yield "dve", 1.4, None, ()
            ready = norm_apply(halves, piece, piece, scaled, NH)
            yield "pe", 1.8, None, ()
            pe.after(identity)
            transposed = []
            for dc in range(DC):
                for j in range(J):
                    pe.after(ready[j])
                    last = nc.tensor.transpose(bank(6 + dc)[:, j * NH:(j + 1) * NH],
                                               ctx[:, j, dc * P:(dc + 1) * P], ident[0:NH, 0:NH])
                transposed.append(pe.did(last))
            yield "act", 1.0, "ctxT", ()
            act.after(cols_in_sb)
            for dc in range(DC):
                act.after(transposed[dc])
                made["ctxT"] = bank_read[6 + dc] = act.did(nc.scalar.activation(
                    ctxT[:, dc, :], bank(6 + dc)[:, 0:J * NH], ACT.Identity, bias=col("lnkv_b", dc),
                    scale=col("lnkv_g", dc)))
            yield "pe", 4.2, None, ()
            pe.after(made["ctxT"], mats_in_sb["wk"])
            k_sum = project(6, lambda c: mat("wk", c), lambda c: ctxT[:, c, :])
            yield "act", 1.1, None, ()
            add_bias(kT, k_sum, 6, "bk")
            yield "pe", 4.2, None, ()
            pe.after(made["bk"], mats_in_sb["wqT"])
            kq_sum = project(6, lambda c: mat("wqT", c), lambda c: kT[:, c, :])
            yield "dve", 0.8, "kq", ()
            dve.after(cols_in_sb)
            for dc in range(DC):
                dve.after(kq_sum[dc])
                made["kq"] = dve.did(nc.vector.tensor_scalar(kq[:, dc, :], bank(6 + dc)[:, 0:J * NH],
                                                             col("lnq_g", dc), None, ALU.mult))
            yield "dve", 0.8, None, ()
            for dc in range(DC):
                made["kq_raw"] = bank_read[6 + dc] = dve.did(nc.vector.tensor_copy(
                    kq_raw[:, dc, :], bank(6 + dc)[:, 0:J * NH]))
            yield "pe", 2.0, None, ()
            pe.after(made["kq_raw"], cols_in_sb)
            pe_bank(6)
            for j in range(J):
                pairs = [(kq_raw, "lnq_b", c) for c in range(DC)] + [(kT, "bq", c) for c in range(DC)]
                for i, (left, name, c) in enumerate(pairs):
                    last = nc.tensor.matmul(bank(6)[0:NH, j:j + 1], left[:, c, j * NH:(j + 1) * NH], col(name, c),
                                            start=i == 0, stop=i == len(pairs) - 1)
            last = pe.did(last)
            yield "dve", 0.2, "qk_bias", ()
            dve.after(last)
            made["qk_bias"] = bank_read[6] = dve.did(nc.vector.tensor_copy(qk_bias[:, :], bank(6)[0:NH, 0:J]))
            yield "dve", 0.6, None, ()
            dve.after(mats_in_sb["w1"])
            for dc in range(DC):
                made["w1g"] = dve.did(nc.vector.tensor_scalar(w1g[:, dc, :], mat("w1", dc), col("lnm_g", dc), None,
                                                              ALU.mult))
            yield "pe", 0.8, None, ()
            pe.after(mats_in_sb["w1"])
            pe_bank(7)
            for fc in range(DC):
                for dc in range(DC):
                    last = nc.tensor.matmul(bank(7)[:, fc:fc + 1], mat("w1", dc)[:, fc * P:(fc + 1) * P],
                                            col("lnm_b", dc), start=dc == 0, stop=dc == DC - 1)
            last = pe.did(last)
            yield "dve", 0.1, None, ()
            dve.after(last)
            made["b1g"] = bank_read[7] = dve.did(nc.vector.tensor_tensor(
                b1g[:, :], bank(7)[:, 0:DC], cols[:, COLS.index("b1"), :], ALU.add))
            yield "dve", 0.8, "mlp", ()
            dve.after(rows_in_sb)
            for b in range(B):
                made["cond"] = dve.did(nc.vector.tensor_tensor(row(f"cond{b}"), row(f"cond{b}"), row("b2"),
                                                               ALU.add))

        def context_values():
            yield "pe", 4.2, None, ["ctxT"]
            pe.after(made["ctxT"], mats_in_sb["wv"])
            v_sum = project(4, lambda c: mat("wv", c), lambda c: ctxT[:, c, :])
            yield "act", 1.1, None, ()
            add_bias(vT, v_sum, 4, "bv")
            for j in range(J):
                i = 4 + j % 2
                yield "pe", 1.7, None, ()
                pe.after(made["bv"], constants, mats_in_sb["wu"])
                pe_bank(i)
                for dc in range(DC):
                    last = nc.tensor.matmul(bank(i)[0:NH, 0:D], vT[:, dc, j * NH:(j + 1) * NH], mat("wu", dc),
                                            start=dc == 0, stop=dc == DC - 1)
                last = pe.did(last)
                yield "dve", 0.4, None, ()
                dve.after(last, rows_in_sb)
                made["values"] = bank_read[i] = dve.did(nc.vector.tensor_tensor(
                    values[:, j, 0:D], bank(i)[0:NH, 0:D], row("bu", NH), ALU.add))
            yield "pe", 3.5, None, ()
            pe.after(made["values"])
            sums = []
            for b in range(B):
                pe_bank(4 + b)
                for h in range(2):
                    last = nc.tensor.matmul(bank(4 + b)[:, 0:D + 1], eps_ones[:, :], values[:, 2 * b + h, 0:D + 1],
                                            start=h == 0, stop=h == 1)
                sums.append(pe.did(last))
            yield "dve", 0.7, "values", ()
            dve.after(pool_constants)
            for b in range(B):
                dve.after(sums[b])
                made["eps_row"] = bank_read[4 + b] = dve.did(nc.vector.tensor_copy(
                    vscaled[b][EPS_ROW:EPS_ROW + 1, 0, 0:D + 1], bank(4 + b)[EPS_ROW:EPS_ROW + 1, 0:D + 1]))

        act.after(first_rows_in_sb)
        expls_ready = act.did(nc.scalar.activation(expls[:, :], row("q_logsig"), ACT.Exp))

        max_ready = [[[None] * Q for _ in range(2)] for _ in range(B)]
        expbias_ready = [[None] * 2 for _ in range(B)]
        exp_done = [[None] * Q for _ in range(B)]
        vscaled_ready = [None] * B

        def evacuate(b, q, marks, banks, dest):
            out_marks = []
            for dc in range(DC):
                act.after(marks[dc])
                m = bank_read[banks[dc]] = act.did(nc.scalar.copy(
                    dest[:, dc, q * BANK:(q + 1) * BANK], bank(banks[dc])))
                out_marks.append(m)
            return out_marks

        def shift_means(tiles, scaled):
            a, z = tiles[0], tiles[-1] + 1
            pool.after(scaled)
            return pool.did(nc.gpsimd.tensor_tensor(shift[:, a:z], neg_mean[:, a:z], rstd[:, a:z], ALU.mult))

        def act_apply(tiles, source, dest, shifted_ready):
            act.after(shifted_ready)
            return [act.did(nc.scalar.activation(dest(g), source(g), ACT.Identity, bias=shift[:, g:g + 1],
                                                 scale=rstd[:, g:g + 1])) for g in tiles]

        def block(b, q):
            tiles = [b * T + q * TQ + i for i in range(TQ)]
            banks = (4 * b + q, 4 * b + 2 + q)
            span = slice(q * BANK, (q + 1) * BANK)
            source = lambda g: slots[:, g, :]
            middle = lambda g: mid[:, g, :]
            hatted = lambda g: hat[:, g, :]
            initial = lambda g: xs[:, g, :]
            yield "dve", 2.0, None, ()
            dve.after(x_in_sb[b, q])
            stats = norm_moments(tiles, initial)
            yield "pool", 1.2, None, ()
            scaled = norm_rstd(tiles, stats)
            yield "dve", 3.45, None, ()
            dve.after(expls_ready, first_rows_in_sb)
            ready = norm_affine(tiles, initial, source, scaled, expls[:, :], row("q_mu"))
            for r in range(ROUNDS):
                yield "act", 2.0, None, ()
                squared = variances(tiles, source, ready)
                yield "pool", 1.5, None, ()
                shifted_ready = rstd_and_shift(tiles, squared)
                yield "act", 2.0, None, ()
                normed = act_apply(tiles, source, hatted, shifted_ready)
                yield "pe", 0.9, None, ["mlp", "values"] if b else ()
                pe.after(identity)
                marks = transpose_block(b, q, hatted, normed, banks)
                yield "act", 1.0, None, ()
                hatT_ready = evacuate(b, q, marks, banks, hatT[b])
                yield "pe", 3.5, None, ["kq"]
                logits_ready = []
                pe.after(made["kq"])
                for h in range(2):
                    j = 2 * b + h
                    pe_bank(banks[h])
                    pe.after(*hatT_ready)
                    for dc in range(DC):
                        last = nc.tensor.matmul(bank(banks[h])[0:NH, :], kq[:, dc, j * NH:(j + 1) * NH],
                                                hatT[b][:, dc, span], start=dc == 0, stop=dc == DC - 1)
                    logits_ready.append(pe.did(last))
                yield "dve", 1.2, ("max", b, q, r), ()
                for h in range(2):
                    dve.after(logits_ready[h])
                    max_ready[b][h][q] = dve.did(nc.vector.reduce_max(
                        rowmax[:, 2 * b + h, q:q + 1], bank(banks[h])[0:NH, :], AX.X))
                if q == 0:
                    yield "dve", 0.77, ("bias", b, r), [("max", b, i, r) for i in range(Q)] + ["qk_bias"]
                    dve.after(made["qk_bias"])
                    for h in range(2):
                        j = 2 * b + h
                        dve.after(*max_ready[b][h])
                        m = dve.did(nc.vector.scalar_tensor_tensor(
                            out=shifted[:, j:j + 1], in0=rowmax[:, j, 0:1], scalar=rowmax[:, j, 1:2],
                            in1=qk_bias[:, j:j + 1], op0=ALU.max, op1=ALU.add))
                        dve.after(m)
                        expbias_ready[b][h] = dve.did(nc.vector.tensor_scalar(
                            expbias[:, j:j + 1], qk_bias[:, j:j + 1], shifted[:, j:j + 1], SHARPEN,
                            ALU.subtract, ALU.mult))
                yield "act exp", 0.97, ("exp", b, q, r), [("bias", b, r)]
                for h in range(2):
                    j = 2 * b + h
                    act.after(expbias_ready[b][h])
                    exp_done[b][q] = bank_read[banks[h]] = act.did(nc.scalar.activation(
                        attn[b][0:NH, h, span], bank(banks[h])[0:NH, :], ACT.Exp, bias=expbias[:, j:j + 1],
                        scale=SHARPEN, accum_out=rowsum[:, j, q:q + 1]))
                if q == 0:
                    yield "dve", 1.0, ("values", b, r), [("exp", b, i, r) for i in range(Q)] + ["values"]
                    dve.after(*exp_done[b])
                    js = slice(2 * b, 2 * b + 2)
                    m = dve.did(nc.vector.tensor_tensor(rowtotal[:, js], rowsum[:, js, 0], rowsum[:, js, 1], ALU.add))
                    dve.after(m)
                    m = dve.did(nc.vector.reciprocal(rrow[:, js], rowtotal[:, js]))
                    dve.after(m)
                    for h in range(2):
                        j = 2 * b + h
                        vscaled_ready[b] = dve.did(nc.vector.tensor_scalar(
                            vscaled[b][0:NH, h, :], values[:, j, :], rrow[:, j:j + 1], None, ALU.mult))
                for i in range(0, TQ, 2):
                    yield "pe", 1.8, None, [("values", b, r)]
                    pe.after(exp_done[b][q], vscaled_ready[b], made["eps_row"])
                    for k in range(2):
                        t = q * TQ + i + k
                        pe_bank(banks[k])
                        for h in range(2):
                            n = EPS_ROW + 1 if h == 0 else NH
                            last = nc.tensor.matmul(bank(banks[k])[:, 0:D + 1], attn[b][0:n, h, t * P:(t + 1) * P],
                                                    vscaled[b][0:n, h, 0:D + 1], start=h == 0, stop=h == 1)
                    attended = pe.did(last)
                    yield "dve", 1.33, None, ()
                    dve.after(attended)
                    for k in range(2):
                        g = tiles[i + k]
                        m = dve.did(nc.vector.reciprocal(rden[:, g:g + 1], bank(banks[k])[:, D:D + 1]))
                    dve.after(m)
                    for k in range(2):
                        g = tiles[i + k]
                        m = bank_read[banks[k]] = dve.did(nc.vector.scalar_tensor_tensor(
                            out=mid[:, g, :], in0=bank(banks[k])[:, 0:D], scalar=rden[:, g:g + 1],
                            in1=slots[:, g, :], op0=ALU.mult, op1=ALU.add, accum_out=total[:, g:g + 1]))
                    added = negative_means(tiles[i:i + 2], m)
                yield "act", 2.0, None, ()
                squared = variances(tiles, middle, added)
                yield "pool", 1.5, None, ()
                shifted_ready = rstd_and_shift(tiles, squared)
                yield "act", 2.0, None, ()
                normed = act_apply(tiles, middle, hatted, shifted_ready)
                yield "pe", 0.9, None, ["mlp"]
                marks = transpose_block(b, q, hatted, normed, banks)
                pool.after(normed[-1], made["cond"])
                conditioned = pool.did(nc.gpsimd.tensor_tensor(
                    mid[:, tiles[0]:tiles[0] + TQ, :], mid[:, tiles[0]:tiles[0] + TQ, :],
                    row(f"cond{b}").rearrange("p (o d) -> p o d", o=1).to_broadcast([P, TQ, D]), ALU.add))
                yield "act", 1.0, None, ()
                hatT_ready = evacuate(b, q, marks, banks, hatT[b])
                yield "pe", 3.5, None, ()
                hidden = []
                pe.after(made["w1g"], mats_in_sb["w2"])
                for fc in range(DC):
                    pe_bank(banks[fc])
                    pe.after(*hatT_ready)
                    for dc in range(DC):
                        last = nc.tensor.matmul(bank(banks[fc]), w1g[:, dc, fc * P:(fc + 1) * P],
                                                hatT[b][:, dc, span], start=dc == 0, stop=dc == DC - 1)
                    hidden.append(pe.did(last))
                yield "act gelu", 0.98, None, ()
                act.after(made["b1g"])
                for fc in range(DC):
                    act.after(hidden[fc])
                    gelu_ready = bank_read[banks[fc]] = act.did(nc.scalar.activation(
                        gel[b][:, fc, span], bank(banks[fc]), ACT.Gelu, bias=b1g[:, fc:fc + 1]))
                yield "pe", 3.5, None, ()
                pe.after(gelu_ready)
                out_ready = []
                for i in range(2):
                    pe_bank(banks[i])
                    for k in range(2):
                        s = (q * TQ + 2 * i + k) * P
                        for fc in range(DC):
                            last = nc.tensor.matmul(bank(banks[i])[:, k * D:(k + 1) * D], gel[b][:, fc, s:s + P],
                                                    mat("w2", fc), start=fc == 0, stop=fc == DC - 1)
                    out_ready.append(pe.did(last))
                yield "dve", 1.4, None, ()
                dve.after(conditioned)
                for i in range(2):
                    g = tiles[2 * i]
                    dve.after(out_ready[i])
                    m = bank_read[banks[i]] = dve.did(nc.vector.tensor_tensor(
                        mid[:, g:g + 2, :], bank(banks[i]).rearrange("p (t d) -> p t d", t=2),
                        mid[:, g:g + 2, :], ALU.add))
                yield "dve", 2.0, None, ()
                dve.after(m)
                stats = norm_moments(tiles, middle)
                yield "pool", 1.0, None, ()
                scaled = norm_rstd(tiles, stats)
                for some in (tiles[:2], tiles[2:]):
                    yield "dve", 1.85, None, ()
                    ready = norm_affine(some, middle, source, scaled, row("lnp_g"), row("lnp_b"))
            yield from route(b, q, tiles, banks, span, ready)

        x1T = attn
        split_ready = [[None] * Q for _ in range(B)]
        x1T_ready = [[None] * Q for _ in range(B)]
        hat_free, mid_free, gel_free = ([[] for _ in range(B)] for _ in range(3))
        weights_stored = [[None] * Q for _ in range(B)]
        for q in range(Q):
            sentinels = dve.did(nc.vector.memset(gscore[q][:, :, EG:], LOW))

        def route(b, q, tiles, banks, span, ready):
            hatted = lambda g: hat[:, g, :]
            summed = lambda g: xs[:, g, :]
            ts = slice(tiles[0], tiles[0] + TQ)
            mid_free[b].append(ready)
            gel_free[b].append(ready)
            yield "dve", 1.2, None, ()
            dve.after(ready)
            added = dve.did(nc.vector.tensor_tensor(xs[:, ts, :], xs[:, ts, :], slots[:, ts, :], ALU.add))
            yield "dve", 2.0, None, ()
            dve.after(added)
            stats = norm_moments(tiles, summed)
            yield "pool", 1.2, None, ()
            shifted_ready = shift_means(tiles, norm_rstd(tiles, stats))
            yield "act", 2.0, None, ()
            normed = act_apply(tiles, summed, hatted, shifted_ready)
            yield "pe", 0.9, None, ()
            marks = transpose_block(b, q, hatted, normed, banks)
            hat_free[b].append(marks[-1])
            yield "act", 2.0, None, ()
            copied = []
            for dc in range(DC):
                act.after(marks[dc])
                act.did(nc.scalar.copy(hatT_hi[b][:, dc, span], bank(banks[dc])))
                m = bank_read[banks[dc]] = act.did(nc.scalar.copy(hatT[b][:, dc, span], bank(banks[dc])))
                copied.append(m)
            yield "pe", 1.6, None, ()
            pe.after(gwT_in_sb, *copied)
            pe_bank(banks[0])
            for i in range(TQ):
                for dc in range(DC):
                    s = (q * TQ + i) * P
                    last = nc.tensor.matmul(bank(banks[0])[:, i * E:(i + 1) * E], hatT[b][:, dc, s:s + P],
                                            gwT[:, dc, :], start=dc == 0, stop=dc == DC - 1)
            gate_ready = pe.did(last)
            yield "act sigmoid", 0.5, None, ()
            act.after(gate_ready)
            scored = bank_read[banks[0]] = act.did(nc.scalar.activation(
                score[:, ts, :], bank(banks[0])[:, 0:TQ * E].rearrange("p (t e) -> p t e", e=E), ACT.Sigmoid))
            yield "dve", 0.21, None, [("chosen", 0, q)] if b else ()
            dve.after(scored, gbias_in_sb, sentinels)
            m = dve.did(nc.vector.tensor_tensor(
                biased[:, ts, :], score[:, ts, :],
                gbias[:, :].rearrange("p (o e) -> p o e", o=1).to_broadcast([P, TQ, E]), ALU.add))
            four = biased[:, ts, :].rearrange("p t (g u v) -> p (t g) u v", g=EG, u=2)
            hi4 = pair_hi[q][:, :, :, :].rearrange("p t g u -> p (t g) u")
            lo4 = pair_lo[q][:, :, :, :].rearrange("p t g u -> p (t g) u")
            top, sec = (a[:, :, :].rearrange("p t g -> p (t g)") for a in (gtop[q], gsec[q]))
            yield "dve", 0.32, None, ()
            dve.after(m)
            dve.did(nc.vector.tensor_tensor(hi4, four[:, :, :, 0], four[:, :, :, 1], ALU.max))
            m = dve.did(nc.vector.tensor_tensor(lo4, four[:, :, :, 0], four[:, :, :, 1], ALU.min))
            yield "dve", 0.32, None, ()
            dve.after(m)
            dve.did(nc.vector.tensor_tensor(top, hi4[:, :, 0], hi4[:, :, 1], ALU.max))
            dve.did(nc.vector.tensor_tensor(sec, hi4[:, :, 0], hi4[:, :, 1], ALU.min))
            m = dve.did(nc.vector.tensor_tensor(lo4[:, :, 0], lo4[:, :, 0], lo4[:, :, 1], ALU.max))
            yield "dve", 0.1, None, ()
            dve.after(m)
            m = dve.did(nc.vector.tensor_tensor(sec, sec, lo4[:, :, 0], ALU.max))
            yield "dve", 0.1, None, ()
            dve.after(m)
            m = dve.did(nc.vector.tensor_tensor(gscore[q][:, :, 0:EG], gtop[q][:, :, :], gsec[q][:, :, :], ALU.add))
            yield "dve", 0.32, None, ()
            dve.after(m)
            for i in range(TQ):
                m = dve.did(nc.vector.max(gbest[q][:, i, :], gscore[q][:, i, :]))
            yield "dve", 0.1, None, ()
            dve.after(m)
            m = dve.did(nc.vector.memset(gbest[q][:, :, TOPG:], LOW))
            yield "dve", 0.32, None, ()
            dve.after(m)
            for i in range(TQ):
                m = dve.did(nc.vector.match_replace(gleft[q][:, i, :], gbest[q][:, i, :], gscore[q][:, i, :],
                                                    STRUCK))
            yield "dve", 0.1, None, ()
            dve.after(m)
            m = dve.did(nc.vector.tensor_tensor(gmask[q][:, :, :], gleft[q][:, :, 0:EG], gscore[q][:, :, 0:EG],
                                                ALU.not_equal))
            yield "dve", 0.21, None, ()
            dve.after(m)
            m = dve.did(nc.vector.tensor_tensor(
                masked[:, ts, :].rearrange("p t (g v) -> p (t g) v", g=EG),
                biased[:, ts, :].rearrange("p t (g v) -> p (t g) v", g=EG),
                gmask[q][:, :, :].rearrange("p t (g o) -> p (t g) o", o=1).to_broadcast([P, TQ * EG, GE]), ALU.mult))
            yield "dve", 0.32, None, ()
            dve.after(m)
            for i in range(TQ):
                m = dve.did(nc.vector.max(ebest[q][:, i, :], masked[:, tiles[i], :]))
            yield "dve", 0.41, None, ()
            dve.after(m)
            for i in range(TQ):
                m = dve.did(nc.vector.match_replace(chosen[:, tiles[i], :], ebest[q][:, i, :],
                                                    masked[:, tiles[i], :], STRUCK))
            yield "dve", 0.21, None, ()
            dve.after(m)
            m = dve.did(nc.vector.tensor_tensor(chosen[:, ts, :], chosen[:, ts, :], masked[:, ts, :],
                                                ALU.not_equal))
            yield "dve", 0.21, None, ()
            dve.after(m)
            m = dve.did(nc.vector.tensor_tensor(chosen[:, ts, :], chosen[:, ts, :], score[:, ts, :], ALU.mult))
            yield "dve", 0.21, None, ()
            dve.after(m)
            m = dve.did(nc.vector.reduce_sum(wsum[q][:, :], chosen[:, ts, :], AX.X))
            yield "dve", 0.1, None, ()
            dve.after(m)
            m = dve.did(nc.vector.tensor_scalar_add(wsum[q][:, :], wsum[q][:, :], 1e-20))
            yield "dve", 0.1, None, ()
            dve.after(m)
            m = dve.did(nc.vector.reciprocal(wnorm[q][:, :], wsum[q][:, :]))
            yield "dve", 0.1, None, ()
            dve.after(m)
            m = dve.did(nc.vector.tensor_scalar(wnorm[q][:, :], wnorm[q][:, :], ROUTE_SCALE, None, ALU.mult))
            yield "dve", 0.21, ("chosen", b, q), ()
            dve.after(m)
            weighed = dve.did(nc.vector.tensor_tensor(
                combine[:, ts, :], chosen[:, ts, :],
                wnorm[q][:, :].rearrange("p (t o) -> p t o", o=1).to_broadcast([P, TQ, E]), ALU.mult))
            yield "pe", 0.9, None, ()
            pe.after(weighed)
            pe_bank(banks[1])
            for i in range(TQ):
                last = nc.tensor.transpose(bank(banks[1])[0:E, i * P:(i + 1) * P], combine[:, tiles[i], :],
                                           ident[:, :])
            turned = pe.did(last)
            yield "act", 0.7, None, ()
            act.after(turned, added)
            combT = part(slots[0:E, ts, :], 0, BANK)
            m = bank_read[banks[1]] = act.did(nc.scalar.copy(combT, bank(banks[1])[0:E, :]))
            sync.after(m)
            s = sem(f"st_comb{b}{q}")
            nc.sync.dma_start(scratch[:, b * S + span.start:b * S + span.stop], combT).then_inc(s, 16)
            weights_stored[b][q] = (s, 16)
            yield "dve", 1.3, None, ()
            for dc in range(DC):
                dve.after(copied[dc])
                split_ready[b][q] = dve.did(nc.vector.tensor_tensor(
                    hatT_lo[b][:, dc, span], hatT[b][:, dc, span], hatT_hi[b][:, dc, span].bitcast(F32),
                    ALU.subtract))
            yield "pe", 0.9, None, ()
            marks = transpose_block(b, q, summed, [added] * TQ, banks)
            yield "act", 1.0, ("routed", b, q), ()
            x1T_ready[b][q] = evacuate(b, q, marks, banks, x1T[b])

        EXPERTS = E + SHARED
        PASSES = (((0, 0),), ((1, 0), (1, 1), (0, 1)))
        PASS_COLUMN = ({(0, 0): 0}, {(0, 1): 0, (1, 0): BANK, (1, 1): 2 * BANK})
        GATE_BANK, UP_BANK = 1, 3
        OUT_BANKS = {(0, 0): (0, 2), (0, 1): (0, 2), (1, 0): (4, 6), (1, 1): (5, 7)}
        order = [(p, e) for p in range(len(PASSES)) for e in range(EXPERTS)]
        work = [(n, b, q) for n, (p, _) in enumerate(order) for b, q in PASSES[p]]
        first_of = [work.index((n, *PASSES[p][0])) for n, (p, _) in enumerate(order)]
        last_of = [f + len(PASSES[p]) - 1 for f, (p, _) in zip(first_of, order)]

        def token_span(b, q):
            return slice(q * BANK, (q + 1) * BANK)

        raw = [part(mid[:, 0:T, :], i * WCOL, WCOL) for i in range(2)]
        raw_sem = [sem(f"ld_w{i}") for i in range(2)]
        raw_read = [None] * 2
        CW = 4
        cw_sem = [sem(f"ld_c{i}") for i in range(CW + 2)]
        cw_loads = [0] * (CW + 2)
        cw_read = [None] * (CW + 2)
        w_loaded, c_loaded, w_ready = {}, {}, {}
        gate_done, up_done, inner_ready, down_done = {}, {}, {}, {}

        def load_weights(n):
            if n >= len(order):
                return
            i = n % 2
            sync.after(*([raw_read[i]] if raw_read[i] else mid_free[0]))
            nc.sync.dma_start(raw[i], experts[order[n][1]]).then_inc(raw_sem[i], 16)
            w_loaded[n] = (raw_sem[i], 16 * (n // 2 + 1))

        def load_routing(n):
            p, e = order[n]
            if p == 0:
                i = e % CW
                slot, tokens = part(gel[0][:, :, :], i * BANK, BANK), slice(0, BANK)
                needed = weights_stored[0][:1] + ([cw_read[i]] if cw_read[i] else gel_free[0])
            else:
                i = CW + e % 2
                slot, tokens = part(gel[1 - e % 2][:, :, :], 0, B * S - BANK), slice(BANK, B * S)
                needed = [m for marks in weights_stored for m in marks]
                needed += ([cw_read[i]] if cw_read[i] else
                           gel_free[1] if e % 2 == 0 else [inner_ready[last_of[EXPERTS - 1]]])
            sync.after(*needed)
            nc.sync.dma_start(slot, scratch[e:e + 1, tokens].to_broadcast([P, tokens.stop - tokens.start]))\
                .then_inc(cw_sem[i], 16)
            cw_loads[i] += 1
            c_loaded[n] = (i, slot, (cw_sem[i], 16 * cw_loads[i]))

        def weights():
            yield "act", 0.1, None, [("routed", 0, 0), ("routed", 0, 1)]
            load_weights(0)
            load_weights(1)
            for n in range(len(order)):
                i = n % 2
                for key, cols, reader, took in (("gate_up", slice(0, 2 * D), up_done, 0.6),
                                                ("down", slice(2 * D, WCOL), down_done, 0.4)):
                    yield "act", took, None, [(key, last_of[n - 2])] if n >= 2 else []
                    act.after(w_loaded[n])
                    if n >= 2:
                        act.after(reader[last_of[n - 2]])
                    hi = act.did(nc.scalar.copy(w_hi[i][:, cols], raw[i][:, cols]))
                    yield "dve", took, ("weights", key, n), ()
                    dve.after(hi, w_loaded[n])
                    w_ready[key, n] = dve.did(nc.vector.tensor_tensor(
                        w_lo[i][:, cols], raw[i][:, cols], w_hi[i][:, cols].bitcast(F32), ALU.subtract))
                raw_read[i] = w_ready["down", n]
                load_weights(n + 2)

        def three_passes(dest, left, right, first, final):
            terms = [(a, c) for (lh, ll), (rh, rl) in zip(left, right) for a, c in ((lh, rh), (lh, rl), (ll, rh))]
            for k, (a, c) in enumerate(terms):
                last = nc.tensor.matmul(dest, a, c, start=first and k == 0, stop=final and k == len(terms) - 1)
            return last

        def gate_up():
            for m, (n, b, q) in enumerate(work):
                hi, lo = w_hi[n % 2], w_lo[n % 2]
                span = token_span(b, q)
                for which, i, done, key in ((0, GATE_BANK, gate_done, "gate"), (1, UP_BANK, up_done, "gate_up")):
                    needs = [("weights", "gate_up", n), ("routed", b, q)]
                    if m:
                        needs.append((("silu", "inner")[which], m - 1))
                    yield "pe", 1.28, (key, m), needs
                    pe.after(w_ready["gate_up", n], split_ready[b][q])
                    pe_bank(i)
                    o = [which * D + dc * P for dc in range(DC)]
                    done[m] = pe.did(three_passes(
                        bank(i), [(hi[:, a:a + P], lo[:, a:a + P]) for a in o],
                        [(hatT_hi[b][:, dc, span], hatT_lo[b][:, dc, span]) for dc in range(DC)], True, True))

        def inner():
            for m, (n, b, q) in enumerate(work):
                p, e = order[n]
                u = m % 2
                ahead = (CW - 1, 1)[p]
                needs = [("gate", m)]
                if p == 1 and e == 0:
                    needs += [("routed", *block) for block in PASSES[p]]
                yield "act silu", 0.48, ("silu", m), needs
                if m == first_of[n]:
                    for k in range(n if e == 0 else n + ahead, n + ahead + 1):
                        if k < len(order) and order[k][0] == p and order[k][1] < E:
                            load_routing(k)
                act.after(gate_done[m], *hat_free[0])
                if m >= 2:
                    act.after(inner_ready[m - 2])
                s = bank_read[GATE_BANK] = act.did(nc.scalar.activation(silu[u], bank(GATE_BANK), ACT.Silu))
                if e < E:
                    yield "dve", 0.6, None, ()
                    i, slot, loaded = c_loaded[n]
                    a = PASS_COLUMN[p][(b, q)]
                    dve.after(s, loaded)
                    s = cw_read[i] = dve.did(nc.vector.tensor_tensor(silu[u], silu[u], slot[:, a:a + BANK],
                                                                     ALU.mult))
                yield "dve", 0.6, ("inner", m), [("gate_up", m)]
                dve.after(s, *hat_free[0])
                dve.after(up_done[m])
                v = bank_read[UP_BANK] = dve.did(nc.vector.tensor_tensor(act_in[u], bank(UP_BANK), silu[u],
                                                                         ALU.mult))
                yield "act", 0.52, None, [("down", m - 2)] if m >= 2 else ()
                act.after(v)
                if m >= 2:
                    act.after(down_done[m - 2])
                h = act.did(nc.scalar.copy(act_hi[u][:, :], act_in[u]))
                yield "dve", 0.6, ("split", m), ()
                dve.after(h)
                inner_ready[m] = dve.did(nc.vector.tensor_tensor(
                    act_lo[u][:, :], act_in[u], act_hi[u][:, :].bitcast(F32), ALU.subtract))

        def down():
            for m, (n, b, q) in enumerate(work):
                p, e = order[n]
                needs = [("split", m), ("weights", "down", n)]
                if n > 0 and m + 1 < len(work) and order[work[m + 1][0]][0] == p:
                    needs.append(("gate_up", m + 1))
                yield "pe", 1.28, ("down", m), needs
                u = m % 2
                pe.after(inner_ready[m], w_ready["down", n])
                chunk_done = []
                for dc in range(DC):
                    i = OUT_BANKS[b, q][dc]
                    if e == 0:
                        pe_bank(i)
                    a = 2 * D + dc * P
                    chunk_done.append(pe.did(three_passes(
                        bank(i), [(w_hi[n % 2][:, a:a + P], w_lo[n % 2][:, a:a + P])],
                        [(act_hi[u][:, :], act_lo[u][:, :])], e == 0, e == EXPERTS - 1)))
                down_done[m] = chunk_done[-1]
                if e == EXPERTS - 1:
                    yield "dve", 1.4, None, ()
                    finish(b, q, chunk_done)

        stored = []

        def finish(b, q, chunk_done):
            span = token_span(b, q)
            dve.after(*x1T_ready[b][q])
            for dc in range(DC):
                i = OUT_BANKS[b, q][dc]
                dve.after(chunk_done[dc])
                m = bank_read[i] = dve.did(nc.vector.tensor_tensor(
                    hatT[b][:, dc, span], bank(i), x1T[b][:, dc, span], ALU.add))
                sync.after(m)
                s = sem(f"st_out{b}{q}{dc}")
                nc.sync.dma_start(out[b, dc, :, span], hatT[b][:, dc, span]).then_inc(s, 16)
                stored.append((s, 16))

        streams = [(context_keys(), 0, 0), (context_values(), 0, 0)]
        streams += [(block(b, q), BLOCK_START_US[b][q], BLOCK_HANDICAP_US[b][q]) for b in range(B) for q in range(Q)]
        streams += [(s(), 0, h) for s, h in zip((weights, down, gate_up, inner), EXPERT_HANDICAP_US)]
        interleave(streams)
        sync.after(*stored)


def kernel(**inputs):
    import numpy as np
    import concourse.bacc as bacc
    from concourse.bass_utils import run_bass_kernel_spmd

    a = {k.replace("L0_xcond_", "").replace("L0_ffn_", ""): np.asarray(v) for k, v in inputs.items()}
    chunked = lambda w: w.reshape(DC, P, -1).transpose(1, 0, 2)
    a["wqT"] = a["wq"].T
    a["cond0"], a["cond1"] = a["cond_1024"]
    mats = np.stack([chunked(a[n]) for n in MATS], axis=1)
    cols = np.stack([a[n].reshape(DC, P).T for n in COLS], axis=1)
    rows = np.concatenate([a[n].reshape(1, D) for n in ROWS], axis=1)

    def expert(gate, up, down):
        return np.concatenate([chunked(gate.T).reshape(P, D), chunked(up.T).reshape(P, D), down.T], axis=1)

    experts = np.stack(
        [expert(a["w_gate"][e], a["w_up"][e], a["w_down"][e]) for e in range(E)]
        + [expert(a["sh_gate"][s:s + I], a["sh_up"][s:s + I], a["sh_down"][:, s:s + I])
           for s in range(0, SHARED * I, I)])
    arrays = {
        "x": a["x"], "ctx": a["ctx_1024"], "rows": rows, "gate_bias": a["gate_bias"].reshape(1, E), "cols": cols,
        "mats": mats, "gate_wT": chunked(a["gate_w"].T), "experts": experts,
    }
    arrays = {k: np.ascontiguousarray(v) for k, v in arrays.items()}
    nc = bacc.Bacc("TRN2", target_bir_lowering=False, num_devices=1)
    args = [nc.dram_tensor(f"in_{n}", v.shape, F32, kind="ExternalInput").ap() for n, v in arrays.items()]
    out = nc.dram_tensor("out", (B, DC, P, S), F32, kind="ExternalOutput").ap()
    scratch = nc.dram_tensor("routing", (E, B * S), F32, kind="Internal").ap()
    build(nc, *args, out, scratch)
    got = run_bass_kernel_spmd(nc, [{f"in_{n}": v for n, v in arrays.items()}], core_ids=[0]).results[0]["out"]
    return np.ascontiguousarray(got.reshape(B, D, S).transpose(0, 2, 1))
```
